# Optimizing a Trainium2 kernel written in Bass

```python
import numpy as np
import jax
import jax.numpy as jnp

def _softmax(x, axis=-1):
    return jax.nn.softmax(x, axis=axis)

def _gelu(x):
    return jax.nn.gelu(x, approximate=True)

def _silu(x):
    return jax.nn.silu(x)

def _sigmoid(x):
    return jax.nn.sigmoid(x)

def _layernorm(x, axis=-1, eps=1e-05):
    m = jnp.mean(x, axis=axis, keepdims=True)
    v = jnp.var(x, axis=axis, keepdims=True)
    return (x - m) / jnp.sqrt(v + eps)

def _scatter_add(tgt, idx, src, axis=0):
    return tgt.at[idx].add(src)

def _segment_sum(src, seg, n):
    return jax.ops.segment_sum(src, seg, n)
kernel_name = 'mk_gnn_resnorm_d2_gnn_r32_95124a'

def setup_inputs(seed: int=0):
    np.random.seed(seed)
    _w = jnp.asarray

    def _rec_inputs():
        import jax
        import jax.numpy as jnp
        _gk = jax.random.key(seed)
        x = -0.0003713 + 1 * jax.random.normal(jax.random.fold_in(_gk, 1), (50000, 128), jnp.float32)
        src = jax.random.randint(jax.random.fold_in(_gk, 2), (50000,), 0, 50000, jnp.int32)
        dst = jax.random.randint(jax.random.fold_in(_gk, 3), (50000,), 0, 50000, jnp.int32)
        _o = jnp.argsort(dst, stable=True)
        src = src[_o]
        dst = dst[_o]
        edge_attr_128 = -6.47781e-05 + 0.999943 * jax.random.normal(jax.random.fold_in(_gk, 13), (50000, 128), jnp.float32)
        return (x, src, dst, edge_attr_128)
    x, src, dst, edge_attr_128 = _rec_inputs()

    def _L0_gnn_setup():
        import jax, jax.numpy as jnp
        import numpy as np
        N_NODES = 3125
        N_EDGES = 50000
        N_NODE_F = 128
        N_EDGE_F = 128
        N_GLOBAL_F = 64
        N_GRAPHS = 256
        HIDDEN = 128
        IN_DIM = N_NODE_F + N_EDGE_F + N_GLOBAL_F
        key = jax.random.key(seed)
        k1, k2, k3, k4, k5, k6 = jax.random.split(key, 6)
        node_feats = jax.random.normal(k1, (N_NODES, N_NODE_F), dtype=jnp.float32)
        edge_feats = jax.random.normal(k2, (N_EDGES, N_EDGE_F), dtype=jnp.float32)
        global_feats = jax.random.normal(k3, (N_GRAPHS, N_GLOBAL_F), dtype=jnp.float32)
        W = jax.random.normal(k4, (HIDDEN, IN_DIM), dtype=jnp.float32) * (1.0 / np.sqrt(IN_DIM))
        edge_index = jax.random.randint(k5, (2, N_EDGES), 0, N_NODES, dtype=jnp.int64)
        batch = jnp.sort(jax.random.randint(k6, (N_NODES,), 0, N_GRAPHS, dtype=jnp.int64))
        return {'node_feats': node_feats, 'edge_feats': edge_feats, 'global_feats': global_feats, 'W': W, 'edge_index': edge_index, 'batch': batch}
    _L0_gnn_all = _L0_gnn_setup()
    _L0_gnn_in = {k: v for k, v in _L0_gnn_all.items() if k in ('global_feats', 'W')}
    del _L0_gnn_all

    def _L1_gnn_setup():
        import jax, jax.numpy as jnp
        import numpy as np
        N = 50000
        D = 128
        H = 8
        DK = D // H
        E = 50000
        L = 2
        LN_EPS = 1e-05

        def _layer_norm(x, g, b):
            m = jnp.mean(x, axis=-1, keepdims=True)
            v = jnp.mean(jnp.square(x - m), axis=-1, keepdims=True)
            return (x - m) * jax.lax.rsqrt(v + LN_EPS) * g + b

        def _gt_layer(h, src, dst, Wq, bq, Wk, bk, Wv, bv, Wo, bo, W1, b1, W2, b2, g1, be1, g2, be2):
            n = h.shape[0]
            Q = (h @ Wq + bq).reshape(n, H, DK)
            K = (h @ Wk + bk).reshape(n, H, DK)
            V = (h @ Wv + bv).reshape(n, H, DK)
            score = jnp.einsum('ehd,ehd->eh', K[src], Q[dst]) / np.sqrt(DK)
            score = jnp.exp(jnp.clip(score, -5.0, 5.0))
            wV = jax.ops.segment_sum(V[src] * score[:, :, None], dst, num_segments=n)
            z = jax.ops.segment_sum(score, dst, num_segments=n)
            attn = wV / (z[:, :, None] + 1e-06)
            h_att = attn.reshape(n, D) @ Wo + bo
            h = _layer_norm(h + h_att, g1, be1)
            ffn = jax.nn.relu(h @ W1 + b1) @ W2 + b2
            h = _layer_norm(h + ffn, g2, be2)
            return h
        key = jax.random.key(seed)
        ks = jax.random.split(key, 16)
        s = 1.0 / np.sqrt(D)
        s2 = 1.0 / np.sqrt(2 * D)
        w = lambda k, shape, sc: jax.random.normal(k, shape, jnp.float32) * sc
        return {'h': jax.random.normal(ks[0], (N, D), jnp.float32), 'src': jax.random.randint(ks[1], (E,), 0, N), 'dst': jax.random.randint(ks[2], (E,), 0, N), 'Wq': w(ks[3], (L, D, D), s), 'bq': jnp.zeros((L, D), jnp.float32), 'Wk': w(ks[4], (L, D, D), s), 'bk': jnp.zeros((L, D), jnp.float32), 'Wv': w(ks[5], (L, D, D), s), 'bv': jnp.zeros((L, D), jnp.float32), 'Wo': w(ks[6], (L, D, D), s), 'bo': jnp.zeros((L, D), jnp.float32), 'W1': w(ks[7], (L, D, 2 * D), s), 'b1': jnp.zeros((L, 2 * D), jnp.float32), 'W2': w(ks[8], (L, 2 * D, D), s2), 'b2': jnp.zeros((L, D), jnp.float32), 'ln1_g': jnp.ones((L, D), jnp.float32), 'ln1_b': jnp.zeros((L, D), jnp.float32), 'ln2_g': jnp.ones((L, D), jnp.float32), 'ln2_b': jnp.zeros((L, D), jnp.float32)}
    _L1_gnn_all = _L1_gnn_setup()
    _L1_gnn_in = {k: v for k, v in _L1_gnn_all.items() if k in ('Wq', 'bq', 'Wk', 'bk', 'Wv', 'bv', 'Wo', 'bo', 'W1', 'b1', 'W2', 'b2', 'ln1_g', 'ln1_b', 'ln2_g', 'ln2_b')}
    del _L1_gnn_all
    return {'x': x, 'src': src, 'dst': dst, 'edge_attr_128': edge_attr_128, 'L0_gnn_global_feats': _L0_gnn_in['global_feats'], 'L0_gnn_W': _L0_gnn_in['W'], 'L1_gnn_Wq': _L1_gnn_in['Wq'], 'L1_gnn_bq': _L1_gnn_in['bq'], 'L1_gnn_Wk': _L1_gnn_in['Wk'], 'L1_gnn_bk': _L1_gnn_in['bk'], 'L1_gnn_Wv': _L1_gnn_in['Wv'], 'L1_gnn_bv': _L1_gnn_in['bv'], 'L1_gnn_Wo': _L1_gnn_in['Wo'], 'L1_gnn_bo': _L1_gnn_in['bo'], 'L1_gnn_W1': _L1_gnn_in['W1'], 'L1_gnn_b1': _L1_gnn_in['b1'], 'L1_gnn_W2': _L1_gnn_in['W2'], 'L1_gnn_b2': _L1_gnn_in['b2'], 'L1_gnn_ln1_g': _L1_gnn_in['ln1_g'], 'L1_gnn_ln1_b': _L1_gnn_in['ln1_b'], 'L1_gnn_ln2_g': _L1_gnn_in['ln2_g'], 'L1_gnn_ln2_b': _L1_gnn_in['ln2_b']}

def reference(x, src, dst, edge_attr_128, L0_gnn_global_feats, L0_gnn_W, L1_gnn_Wq, L1_gnn_bq, L1_gnn_Wk, L1_gnn_bk, L1_gnn_Wv, L1_gnn_bv, L1_gnn_Wo, L1_gnn_bo, L1_gnn_W1, L1_gnn_b1, L1_gnn_W2, L1_gnn_b2, L1_gnn_ln1_g, L1_gnn_ln1_b, L1_gnn_ln2_g, L1_gnn_ln2_b):
    import jax
    import jax.numpy as jnp

    def _L0_gnn_ref(node_feats, edge_feats, global_feats, W, edge_index, batch):
        import jax, jax.numpy as jnp
        import numpy as np
        N_NODES = 3125
        N_EDGES = 50000
        N_NODE_F = 128
        N_EDGE_F = 128
        N_GLOBAL_F = 64
        N_GRAPHS = 256
        HIDDEN = 128
        IN_DIM = N_NODE_F + N_EDGE_F + N_GLOBAL_F
        n_nodes = node_feats.shape[0]
        idx_dst = edge_index[1]
        sums = jax.ops.segment_sum(edge_feats, idx_dst, num_segments=n_nodes)
        counts = jax.ops.segment_sum(jnp.ones((edge_feats.shape[0],), dtype=edge_feats.dtype), idx_dst, num_segments=n_nodes)
        mean_edge = sums / jnp.maximum(counts, 1.0)[:, None]
        out = jnp.concatenate([node_feats, mean_edge, global_feats[batch]], axis=1)
        h = jnp.einsum('ni,oi->no', out, W)
        return jax.nn.softplus(h) - jnp.log(jnp.asarray(2.0, dtype=h.dtype))

    def _L1_gnn_ref(h, src, dst, Wq, bq, Wk, bk, Wv, bv, Wo, bo, W1, b1, W2, b2, ln1_g, ln1_b, ln2_g, ln2_b):
        import jax, jax.numpy as jnp
        import numpy as np
        N = 50000
        D = 128
        H = 8
        DK = D // H
        E = 50000
        L = 2
        LN_EPS = 1e-05

        def _layer_norm(x, g, b):
            m = jnp.mean(x, axis=-1, keepdims=True)
            v = jnp.mean(jnp.square(x - m), axis=-1, keepdims=True)
            return (x - m) * jax.lax.rsqrt(v + LN_EPS) * g + b

        def _gt_layer(h, src, dst, Wq, bq, Wk, bk, Wv, bv, Wo, bo, W1, b1, W2, b2, g1, be1, g2, be2):
            n = h.shape[0]
            Q = (h @ Wq + bq).reshape(n, H, DK)
            K = (h @ Wk + bk).reshape(n, H, DK)
            V = (h @ Wv + bv).reshape(n, H, DK)
            score = jnp.einsum('ehd,ehd->eh', K[src], Q[dst]) / np.sqrt(DK)
            score = jnp.exp(jnp.clip(score, -5.0, 5.0))
            wV = jax.ops.segment_sum(V[src] * score[:, :, None], dst, num_segments=n)
            z = jax.ops.segment_sum(score, dst, num_segments=n)
            attn = wV / (z[:, :, None] + 1e-06)
            h_att = attn.reshape(n, D) @ Wo + bo
            h = _layer_norm(h + h_att, g1, be1)
            ffn = jax.nn.relu(h @ W1 + b1) @ W2 + b2
            h = _layer_norm(h + ffn, g2, be2)
            return h
        for l in range(L):
            h = _gt_layer(h, src, dst, Wq[l], bq[l], Wk[l], bk[l], Wv[l], bv[l], Wo[l], bo[l], W1[l], b1[l], W2[l], b2[l], ln1_g[l], ln1_b[l], ln2_g[l], ln2_b[l])
        return h
    edge_index = jnp.stack([src, dst])
    batch0 = jnp.zeros((50000,), jnp.int32)
    x = _layernorm(x + _L0_gnn_ref(x, edge_attr_128, L0_gnn_global_feats, L0_gnn_W, edge_index, batch0), axis=-1)
    x = _layernorm(x + _L1_gnn_ref(x, src, dst, L1_gnn_Wq, L1_gnn_bq, L1_gnn_Wk, L1_gnn_bk, L1_gnn_Wv, L1_gnn_bv, L1_gnn_Wo, L1_gnn_bo, L1_gnn_W1, L1_gnn_b1, L1_gnn_W2, L1_gnn_b2, L1_gnn_ln1_g, L1_gnn_ln1_b, L1_gnn_ln2_g, L1_gnn_ln2_b), axis=-1)
    return x

_drawn_inputs = setup_inputs


def setup_inputs(seed=0):
    import zlib

    import numpy as np

    out = dict(_drawn_inputs(seed))
    spreads = {'L1_gnn_bq': (0.0, 0.687),
     'L1_gnn_bk': (0.0, 0.8),
     'L1_gnn_bv': (0.0, 0.1),
     'L1_gnn_bo': (0.0, 0.1),
     'L1_gnn_b1': (0.0, 0.1),
     'L1_gnn_b2': (0.0, 0.1),
     'L1_gnn_ln1_g': (1.0, 0.2),
     'L1_gnn_ln1_b': (0.0, 0.1),
     'L1_gnn_ln2_g': (1.0, 0.2),
     'L1_gnn_ln2_b': (0.0, 0.1)}
    factors = {}
    for name, (base, spread) in spreads.items():
        noise = np.random.default_rng([zlib.crc32(name.encode()), seed]).standard_normal(out[name].shape)
        drawn = base * np.exp(spread * noise) if base else spread * noise
        out[name] = jnp.asarray(drawn.astype(out[name].dtype))
    for name, factor in factors.items():
        out[name] = (out[name] * factor).astype(out[name].dtype)
    return out
```

```python
from collections import namedtuple
from contextlib import ExitStack
import math

import concourse.bass as bass
from concourse import mybir

F32 = mybir.dt.float32
I32 = mybir.dt.int32
ALU = mybir.AluOpType
ACT = mybir.ActivationFunctionType

NODES = 50000
D = 128
HEADS = 8
DK = D // HEADS
LAYERS = 2
T = 4
ROWS = 128 * T
FULL = NODES // ROWS
TAIL = (NODES - FULL * ROWS) // T
GROUPS = FULL + 1
PAD = (GROUPS + 1) * ROWS
DUMP = GROUPS * ROWS
WM = D + 1
WA = D + HEADS
EPS = 1e-5

assert NODES == FULL * ROWS + TAIL * T and GROUPS % 2 == 0

Group = namedtuple("Group", "n h u P")


def near(g, d):
    k = g.u + d
    n = g.n + d
    if isinstance(n, int):
        if n < 0 or n >= GROUPS:
            return None
        return Group(n, n // 2, n % 2, TAIL if n == FULL else 128)
    return Group(n, g.h + k // 2, k % 2, 128)


def from_group(g, k):
    return not isinstance(g.n, int) or g.n >= k


def over_groups(eng, step):
    def peeled(n):
        step(Group(n, n // 2, n % 2, TAIL if n == FULL else 128))

    for n in range(4):
        peeled(n)
    with eng.Fori(2, (GROUPS - 4) // 2) as h:
        for u in range(2):
            step(Group(h * 2 + u, h, u, 128))
    for n in range((GROUPS - 4) // 2 * 2, GROUPS):
        peeled(n)


def rows_of(dram, g, width):
    if isinstance(g.n, int) and g.n == FULL:
        part = dram[FULL * ROWS:NODES, :]
        return part.rearrange("(p c) f -> p (c f)", c=T)
    full = dram[0:FULL * ROWS, :].rearrange("(g p c) f -> g p (c f)", p=128, c=T)
    return full[g.n, :, :]


def tiles(t, P):
    return t[0:P, :].rearrange("p (c f) -> p c f", c=T)


def program(nc, a, out):
    with ExitStack() as ctx:
        buffers = {}

        def sb(name, shape, dt=F32):
            if name not in buffers:
                buffers[name] = ctx.enter_context(nc.sbuf_tensor(name, shape, dt))
            return buffers[name]

        def gpsimd_pair(name):
            return [ctx.enter_context(nc.semaphore(f"{name}{u}")) for u in range(2)]

        e_scattered = gpsimd_pair("e_scattered")
        a_gathered = [gpsimd_pair(f"a{l}_gathered") for l in range(LAYERS)]
        a_scattered = [gpsimd_pair(f"a{l}_scattered") for l in range(LAYERS)]
        nc.all_engine_barrier()
        first_num = nc.alloc_semaphore(name="first")
        nc.release_semaphore(first_num)

        def semaphores(phase, prefix=""):
            made = []

            def sem(name):
                made.append(phase.enter_context(nc.semaphore(prefix + name, num=first_num.num + len(made))))
                return made[-1]

            def pair(name):
                return [sem(f"{name}0"), sem(f"{name}1")]

            phase.callback(lambda: nc.all_engine_barrier(sems_to_clear=range(made[0].num, made[-1].num + 1)))
            return sem, pair

        def dram(name, rows, width):
            return nc.dram_tensor(name, (rows, width), F32, kind="Internal").ap()

        edge_sum = dram("edge_sum", PAD, WM)
        attn_sum = [dram(f"attn_sum{l}", PAD, WA) for l in range(LAYERS)]
        x1 = dram("x1", NODES, D)
        h1 = dram("h1", NODES, D)

        banks = ctx.enter_context(nc.psum_tensor("banks", [128, 8, 512], F32))

        ident = sb("ident", [128, 128])
        early = sb("early", [128, T, 128])
        zeros = sb("zeros", [128, T * WA])
        ones = sb("ones", [128, 128])
        heads = sb("heads", [128, HEADS])
        dumprow = sb("dumprow", [128, T])
        eps = sb("eps", [128, 1])
        w0 = sb("w0", [128, 320])
        wxT = sb("wxT", [128, 128])
        weT = sb("weT", [128, 128])
        wgT = sb("wgT", [64, 128])
        glob = sb("glob", [64, 1])
        gvec = sb("gvec", [128, 1])
        wq, wk, wv, wo = (sb(f"w{n}", [128, LAYERS, 128]) for n in "qkvo")
        w1 = sb("w1", [128, LAYERS, 256])
        w2 = sb("w2", [128, LAYERS, 2, 128])
        bq, bk, b2, g1, be1 = (sb(n, [128, LAYERS]) for n in ("bq", "bk", "b2", "g1", "be1"))
        b1 = sb("b1", [128, LAYERS * 2])
        bv = sb("bv", [1, LAYERS, 128])
        bo, g2, be2 = (sb(n, [128, LAYERS, 128]) for n in ("bo", "g2", "be2"))
        srcs, dsts, tgts = (sb(n, [128, GROUPS * T], I32) for n in ("srcs", "dsts", "tgts"))
        dstf = sb("dstf", [128, GROUPS * T])

        with ExitStack() as c2:
            sem, pair = semaphores(c2)
            s_const = sem("setup_const")
            s_w0 = sem("setup_w0")
            s_idx = sem("setup_idx")
            s_ld = sem("setup_loads")
            s_zero = sem("setup_zero")
            s_clear = sem("setup_clear")
            s_t = sem("setup_wT")
            s_tc = sem("setup_wT_copied")
            s_gv = sem("setup_gvec")
            s_masks = sem("setup_masks")
            s_done = sem("setup_dve")
            loads = [
                (wq[:, :, :], a["Wq"].rearrange("l k m -> k l m")), (wk[:, :, :], a["Wk"].rearrange("l k m -> k l m")),
                (wv[:, :, :], a["Wv"].rearrange("l k m -> k l m")), (wo[:, :, :], a["Wo"].rearrange("l k m -> k l m")),
                (w1[:, :, :], a["W1"].rearrange("l k m -> k l m")),
                (bv[:, :, :], a["bv"].rearrange("(a l) d -> a l d", a=1)),
            ]
            loads += [(w2[:, l, :, :], a["W2"][l, :, :].rearrange("(c k) m -> k c m", k=128)) for l in range(LAYERS)]
            loads += [(t[:, l:l + 1], a[n][l, :].rearrange("(d a) -> d a", a=1)) for t, n in
                      ((bq, "bq"), (bk, "bk"), (b2, "b2"), (g1, "ln1_g"), (be1, "ln1_b")) for l in range(LAYERS)]
            loads += [(b1[:, 2 * l + k:2 * l + k + 1], a["b1"][l, 128 * k:128 * (k + 1)].rearrange("(d a) -> d a", a=1))
                      for l in range(LAYERS) for k in range(2)]
            loads += [(t[:, l, :], a[n][l, :].partition_broadcast(128)) for t, n in
                      ((bo, "bo"), (g2, "ln2_g"), (be2, "ln2_b")) for l in range(LAYERS)]
            block = c2.enter_context(nc.Block())

            @block.sync
            def _(sp):
                sp.dma_start(w0[:, :], a["W"]).then_inc(s_w0, 16)
                sp.dma_start(glob[:, :], a["glob"][0, :].rearrange("(k a) -> k a", a=1)).then_inc(s_w0, 16)
                sp.wait_ge(s_clear, 3)
                for t, n in ((dsts, "dst"), (srcs, "src")):
                    full = a[n][0:FULL * ROWS].rearrange("(g p c) -> p g c", p=128, c=T)
                    sp.dma_start(t[:, 0:FULL * T].rearrange("p (g c) -> p g c", c=T), full).then_inc(s_idx, 16)
                    sp.dma_start(t[0:TAIL, FULL * T:], a[n][FULL * ROWS:NODES].rearrange("(p c) -> p c", c=T))\
                      .then_inc(s_idx, 16)
                for to, fr in loads:
                    sp.dma_start(to, fr).then_inc(s_ld, 16)
                sp.wait_ge(s_ld, 16 * len(loads))
                sp.wait_ge(s_zero, 16 * (GROUPS + 1))

            @block.scalar
            def _(act):
                act.wait_ge(s_clear, 1)
                for g in range(GROUPS + 1):
                    act.dma_start(edge_sum[g * ROWS:(g + 1) * ROWS, :].rearrange("(p c) f -> p (c f)", c=T),
                                  zeros[:, 0:T * WM]).then_inc(s_zero, 16)

            @block.gpsimd
            def _(pool):
                pool.memset(ident[:, :], 0.0).then_inc(s_const, 1)
                pool.memset(early[:, :, :], 1.0).then_inc(s_const, 1)
                pool.memset(heads[:, :], DK ** -0.5).then_inc(s_const, 1)
                pool.memset(ones[:, :], 1.0).then_inc(s_const, 1)
                pool.memset(eps[:, :], EPS).then_inc(s_const, 1)
                pool.iota(dumprow[:, :], pattern=[[128, T]], base=DUMP, channel_multiplier=1,
                          allow_small_or_imprecise_dtypes=True).then_inc(s_const, 1)
                pool.wait_ge(s_const, 6)
                pool.affine_select(out=ident[:, :], in_=ident[:, :], compare_op=ALU.not_equal, fill=1.0, base=0,
                                   pattern=[[-1, 128]], channel_multiplier=1).then_inc(s_masks, 1)
                pool.affine_select(out=early[:, 3, :], in_=early[:, 3, :], compare_op=ALU.is_gt, fill=0.0, base=0,
                                   pattern=[[-1, 128]], channel_multiplier=1).then_inc(s_masks, 1)
                pool.affine_select(out=heads[:, :], in_=heads[:, :], compare_op=ALU.is_ge, fill=0.0, base=0,
                                   pattern=[[-DK, HEADS]], channel_multiplier=1).then_inc(s_masks, 1)
                pool.wait_ge(s_masks, 3)
                pool.affine_select(out=heads[:, :], in_=heads[:, :], compare_op=ALU.is_ge, fill=0.0, base=DK - 1,
                                   pattern=[[DK, HEADS]], channel_multiplier=-1).then_inc(s_masks, 1)

            @block.vector
            def _(dve):
                dve.memset(zeros[:, :], 0.0).then_inc(s_clear, 1)
                dve.memset(srcs[:, :], 0.0).then_inc(s_clear, 1)
                dve.memset(dsts[:, :], 0.0).then_inc(s_clear, 1)
                dve.memset(tgts[:, :], 0.0).then_inc(s_done, 1)
                for k, (t, n) in enumerate(((wxT, 128), (weT, 128), (wgT, 64))):
                    dve.wait_ge(s_t, k + 1)
                    dve.tensor_copy(t[:, :], banks[0:n, k, 0:128]).then_inc(s_tc, 1)
                dve.wait_ge(s_gv, 1)
                dve.tensor_copy(gvec[:, :], banks[:, 3, 0:1]).then_inc(s_done, 1)
                dve.wait_ge(s_idx, 64)
                dve.tensor_copy(dstf[:, :], dsts[:, :]).then_inc(s_done, 1)

            @block.tensor
            def _(pe):
                pe.wait_ge(s_w0, 32)
                pe.wait_ge(s_masks, 1)
                for k, n in enumerate((128, 128, 64)):
                    pe.transpose(banks[0:n, k, 0:128], w0[:, 128 * k:128 * k + n], ident[:, :]).then_inc(s_t, 1)
                pe.wait_ge(s_tc, 3)
                pe.matmul(banks[:, 3, 0:1], wgT[:, :], glob[:, :], start=True, stop=True).then_inc(s_gv, 1)

        nudge = sb("nudge", [128, 8])

        def carry_wait(eng, g, col, used):
            if from_group(g, 1):
                eng.wait_ge(used, g.n)
            eng.tensor_tensor(nudge[:, col:col + 1], ones[:, 0:1], ones[:, 0:1], ALU.mult).then_inc(used, 1)

        dcol = [sb(f"dcol{u}", [128, T]) for u in range(2)]
        same = [sb(f"same{u}", [128, T, T, 128]) for u in range(2)]
        tgt = [sb(f"tgt{u}", [128, T], I32) for u in range(2)]

        def copy_dst(dve, g, ready):
            dve.tensor_copy(dcol[g.u][0:g.P, :], dstf[0:g.P, bass.ds(g.n * T, T)]).then_inc(ready, 1)

        def spread_dst(pe, g, bank, ready):
            P = g.P
            for c in range(T):
                last = pe.transpose(bank[0:P, c * 128:c * 128 + P], dcol[g.u][0:P, c:c + 1].to_broadcast([P, P]),
                                    ident[0:P, 0:P])
            last.then_inc(ready, 1)

        def build_same(dve, g, bank, ready):
            P = g.P
            seen = tiles(bank, P)[:, :, 0:P]
            for c in range(T):
                dve.tensor_scalar(same[g.u][0:P, c, :, 0:P], seen, dcol[g.u][0:P, c:c + 1], None, ALU.is_equal)\
                   .then_inc(ready, 1)

        def sum_same(pe, g, rows, width, sums, ready):
            P = g.P
            for b in range(T):
                to = sums[0:P, b // 2, (b % 2) * width:(b % 2 + 1) * width]
                for c in range(T):
                    last = pe.matmul(to, same[g.u][0:P, c, b, 0:P], rows[0:P, c, 0:width],
                                     start=(c == 0), stop=(c == T - 1))
            last.then_inc(ready, 1)

        with ExitStack() as c2:
            sem, pair = semaphores(c2)
            feat = [sb(f"feat{u}", [128, T, WM]) for u in range(2)]
            sums = [sb(f"esums{u}", [128, T * WM]) for u in range(2)]
            junk = sb("junk", [128, T, 128])
            before = [sb(f"before{u}", [128, T]) for u in range(2)]
            away = sb("away", [128, T])
            shift = sb("shift", [128, T])
            s_one = sem("e_ones")
            s_feat = pair("e_feat")
            s_dcol = sem("e_dcol")
            s_spread = sem("e_spread")
            s_same = sem("e_same")
            s_before = sem("e_before")
            s_away = sem("e_away")
            s_shift = sem("e_shift")
            s_tgt = sem("e_tgt")
            s_keep = sem("e_keep")
            s_mm = sem("e_summed")
            s_sums = sem("e_sums")
            s_scat = e_scattered
            s_zero = pair("e_zeroed")
            s_carry = sem("e_carry")
            block = c2.enter_context(nc.Block())

            @block.sync
            def _(sp):
                sp.wait_ge(s_one, 2)

                def step(g):
                    if from_group(g, 2):
                        sp.wait_ge(s_mm, g.n - 1)
                    src = rows_of(a["edge"], g, D).rearrange("p (c f) -> p c f", c=T)
                    sp.dma_start(feat[g.u][0:g.P, :, 0:D], src).then_inc(s_feat[g.u], 16)
                over_groups(sp, step)

            @block.scalar
            def _(act):
                def zero(g):
                    for l in range(LAYERS):
                        part = attn_sum[l].rearrange("(g p c) f -> g p (c f)", p=128, c=T)[g.n, :, :]
                        act.dma_start(part, zeros[:, :]).then_inc(s_zero[g.u], 16)

                def step(g):
                    zero(g)
                    act.wait_ge(s_mm, g.n + 1)
                    if from_group(g, 2):
                        act.wait_ge(s_scat[g.u], g.h * (16 * T))
                    act.activation(sums[g.u][0:g.P, :].rearrange("p (k f) -> p k f", k=2),
                                   banks[0:g.P, 2 + 2 * g.u:4 + 2 * g.u, 0:2 * WM], ACT.Copy).then_inc(s_sums, 1)
                over_groups(act, step)
                zero(Group(GROUPS, GROUPS // 2, 0, 128))
                act.wait_ge(s_zero[0], 32 * (GROUPS // 2 + 1))
                act.wait_ge(s_zero[1], 32 * (GROUPS // 2))

            @block.gpsimd
            def _(pool):
                def step(g):
                    pool.wait_ge(s_tgt, g.n + 1)
                    pool.wait_ge(s_sums, g.n + 1)
                    if from_group(g, 1):
                        p = near(g, -1)
                        pool.wait_ge(s_scat[p.u], (p.h + 1) * (16 * T))
                    carry_wait(pool, g, 0, s_carry)
                    for c in range(T):
                        pool.indirect_dma_start(edge_sum, bass.IndirectOffsetOnAxis(tgt[g.u][0:g.P, c:c + 1], 0),
                                                sums[g.u][0:g.P, c * WM:(c + 1) * WM], None, compute_op=ALU.add)\
                            .then_inc(s_scat[g.u], 16)
                over_groups(pool, step)
                pool.wait_ge(s_scat[0], GROUPS // 2 * 16 * T)
                pool.wait_ge(s_scat[1], GROUPS // 2 * 16 * T)

            @block.vector
            def _(dve):
                for u in range(2):
                    dve.memset(feat[u][:, :, D:WM], 1.0).then_inc(s_one, 1)
                copy_dst(dve, Group(0, 0, 0, 128), s_dcol)

                def step(g):
                    nxt = near(g, 1)
                    if nxt:
                        if from_group(g, 1):
                            dve.wait_ge(s_keep, g.n)
                            dve.wait_ge(s_spread, g.n)
                        copy_dst(dve, nxt, s_dcol)
                    dve.wait_ge(s_spread, g.n + 1)
                    dve.wait_ge(s_dcol, g.n + 1)
                    if from_group(g, 2):
                        dve.wait_ge(s_mm, g.n - 1)
                    bank = banks[:, g.u, :]
                    build_same(dve, g, bank, s_same)
                    P = g.P
                    for c in range(T):
                        if c or from_group(g, 1):
                            dve.wait_ge(s_before, g.n * T + c)
                        dve.scalar_tensor_tensor(out=junk[0:P, 0:c + 1, 0:P], in0=tiles(bank, P)[:, 0:c + 1, 0:P],
                                                 scalar=dcol[g.u][0:P, c:c + 1], in1=early[0:P, T - 1 - c:T, 0:P],
                                                 op0=ALU.is_equal, op1=ALU.mult,
                                                 accum_out=before[g.u][0:P, c:c + 1]).then_inc(s_before, 1)
                    if from_group(g, 1):
                        dve.wait_ge(s_shift, g.n)
                    dve.tensor_tensor(away[0:P, :], dumprow[0:P, :], dcol[g.u][0:P, :], ALU.subtract)\
                       .then_inc(s_away, 1)
                    dve.wait_ge(s_away, g.n + 1)
                    dve.wait_ge(s_before, (g.n + 1) * T)
                    if from_group(g, 1):
                        dve.wait_ge(s_tgt, g.n)
                    dve.scalar_tensor_tensor(out=shift[0:P, :], in0=before[g.u][0:P, :], scalar=1.0,
                                             in1=away[0:P, :], op0=ALU.min, op1=ALU.mult).then_inc(s_shift, 1)
                    dve.wait_ge(s_shift, g.n + 1)
                    if from_group(g, 2):
                        dve.wait_ge(s_scat[g.u], g.h * (16 * T))
                    dve.tensor_tensor(tgt[g.u][0:P, :], shift[0:P, :], dcol[g.u][0:P, :], ALU.add).then_inc(s_tgt, 1)
                    dve.wait_ge(s_tgt, g.n + 1)
                    dve.tensor_copy(tgts[0:P, bass.ds(g.n * T, T)], tgt[g.u][0:P, :]).then_inc(s_keep, 1)
                over_groups(dve, step)

            @block.tensor
            def _(pe):
                def spread(g):
                    pe.wait_ge(s_dcol, g.n + 1)
                    if from_group(g, 2):
                        pe.wait_ge(s_keep, g.n - 1)
                    spread_dst(pe, g, banks[:, g.u, :], s_spread)

                spread(Group(0, 0, 0, 128))

                def step(g):
                    if near(g, 1):
                        spread(near(g, 1))
                    pe.wait_ge(s_same, (g.n + 1) * T)
                    pe.wait_ge(s_feat[g.u], (g.h + 1) * 16)
                    if from_group(g, 2):
                        pe.wait_ge(s_sums, g.n - 1)
                    sum_same(pe, g, feat[g.u], WM, banks[:, 2 + 2 * g.u:4 + 2 * g.u, :], s_mm)
                over_groups(pe, step)

        class Norm:

            def __init__(self, sem, name, kind):
                self.col = 1 + kind
                self.st = sb(f"norm{kind}st", [128, T, 6])
                self.mv = sb(f"norm{kind}mv", [128, T, 2])
                self.sd, self.rs, self.t1, self.t2 = (sb(f"norm{kind}{n}", [128, T]) for n in ("sd", "rs", "t1", "t2"))
                self.s_carry = sem(name + "_carry")
                self.s_st = sem(name + "_stats")
                self.s_mv = sem(name + "_meanvar")
                self.s_ln = sem(name + "_lnvar")
                self.s_sd = sem(name + "_root")
                self.s_t1 = sem(name + "_newton1")
                self.s_t2 = sem(name + "_newton2")
                self.s_rs = sem(name + "_rstd")
                self.s_out = sem(name + "_normed")

        def norm_stats(dve, N, g, y):
            P = g.P
            if from_group(g, 1):
                dve.wait_ge(N.s_out, g.n)
            for c in range(T):
                last = dve.bn_stats(N.st[0:P, c, :], y[:, c, :])
            last.then_inc(N.s_st, 1)
            dve.wait_ge(N.s_st, g.n + 1)
            carry_wait(dve, g, N.col, N.s_carry)
            for c in range(T):
                last = dve.bn_aggr(N.mv[0:P, c, :], N.st[0:P, c, :])
            last.then_inc(N.s_mv, 1)

        def norm_root(act, N, g):
            act.wait_ge(N.s_mv, g.n + 1)
            if from_group(g, 1):
                act.wait_ge(N.s_rs, g.n)
            act.activation(N.sd[0:g.P, :], N.mv[0:g.P, :, 1], ACT.Sqrt, bias=eps[0:g.P, :]).then_inc(N.s_sd, 1)

        def norm_recip(dve, N, g):
            dve.wait_ge(N.s_sd, g.n + 1)
            dve.reciprocal(N.rs[0:g.P, :], N.sd[0:g.P, :]).then_inc(N.s_rs, 1)

        def norm_root_exp(act, N, g):
            act.wait_ge(N.s_mv, g.n + 1)
            if from_group(g, 1):
                act.wait_ge(N.s_rs, g.n)
            act.activation(N.t1[0:g.P, :], N.mv[0:g.P, :, 1], ACT.Ln, bias=eps[0:g.P, :]).then_inc(N.s_ln, 1)
            act.wait_ge(N.s_ln, g.n + 1)
            act.activation(N.sd[0:g.P, :], N.t1[0:g.P, :], ACT.Exp, scale=-0.5).then_inc(N.s_sd, 1)

        def norm_newton(dve, N, g):
            P = g.P
            dve.wait_ge(N.s_sd, g.n + 1)
            dve.scalar_tensor_tensor(out=N.t2[0:P, :], in0=N.mv[0:P, :, 1], scalar=EPS, in1=N.sd[0:P, :],
                                     op0=ALU.add, op1=ALU.mult).then_inc(N.s_t1, 1)
            dve.wait_ge(N.s_t1, g.n + 1)
            dve.scalar_tensor_tensor(out=N.t2[0:P, :], in0=N.t2[0:P, :], scalar=-0.5, in1=N.sd[0:P, :],
                                     op0=ALU.mult, op1=ALU.mult).then_inc(N.s_t2, 1)
            dve.wait_ge(N.s_t2, g.n + 1)
            dve.scalar_tensor_tensor(out=N.rs[0:P, :], in0=N.t2[0:P, :], scalar=1.5, in1=N.sd[0:P, :],
                                     op0=ALU.add, op1=ALU.mult).then_inc(N.s_rs, 1)

        def norm_apply(dve, N, g, y, to):
            P = g.P
            dve.wait_ge(N.s_rs, g.n + 1)
            for c in range(T):
                last = dve.tensor_scalar(to[:, c, :], y[:, c, :], N.mv[0:P, c, 0:1], N.rs[0:P, c:c + 1],
                                         ALU.subtract, ALU.mult)
            last.then_inc(N.s_out, 1)

        with ExitStack() as c2:
            sem, pair = semaphores(c2)
            xr = [sb(f"xr{u}", [128, T, D]) for u in range(2)]
            es = [sb(f"es{u}", [128, T, WM]) for u in range(2)]
            cnt = sb("cnt", [128, T])
            rc = sb("rc", [128, T])
            mean = sb("mean", [128, T, D])
            xT = sb("xT", [128, 512])
            mT = sb("mT", [128, 512])
            ab = sb("ab", [128, 512])
            ex = sb("ex", [128, 512])
            pos = sb("pos", [128, 512])
            sp_ = [sb(f"softp{u}", [128, 512]) for u in range(2)]
            y = sb("y", [128, T, D])
            o = [sb(f"o{u}", [128, T, D]) for u in range(2)]
            N = Norm(sem, "n0", 1)
            s_x, s_es, s_st = pair("z_x"), pair("z_es"), pair("z_stored")
            s_cnt, s_rc, s_mean = sem("z_cnt"), sem("z_rc"), sem("z_mean")
            s_xt, s_mt, s_xT, s_mT = sem("z_xt"), sem("z_mt"), sem("z_xT"), sem("z_mT")
            s_h, s_ab, s_ex, s_lg = sem("z_h"), sem("z_abs"), sem("z_exp"), sem("z_log")
            s_pos, s_soft, s_back, s_y = sem("z_pos"), sem("z_soft"), sem("z_back"), sem("z_y")
            block = c2.enter_context(nc.Block())
            PX, PM, PH, PL, PB = 0, 1, 2, 3, 4

            @block.sync
            def _(sp):
                def step(g):
                    if from_group(g, 2):
                        sp.wait_ge(s_mean, g.n - 1)
                    sp.dma_start(es[g.u][0:g.P, :, :], rows_of(edge_sum, g, WM).rearrange("p (c f) -> p c f", c=T))\
                      .then_inc(s_es[g.u], 16)
                    if from_group(g, 2):
                        sp.wait_ge(s_y, g.n - 1)
                    sp.dma_start(xr[g.u][0:g.P, :, :], rows_of(a["x"], g, D).rearrange("p (c f) -> p c f", c=T))\
                      .then_inc(s_x[g.u], 16)
                    p = near(g, -2)
                    if p:
                        store(p)

                def store(g):
                    sp.wait_ge(N.s_out, g.n + 1)
                    sp.dma_start(rows_of(x1, g, D), o[g.u][0:g.P, :, :].rearrange("p c f -> p (c f)"))\
                      .then_inc(s_st[g.u], 16)
                over_groups(sp, step)
                for n in (GROUPS - 2, GROUPS - 1):
                    store(Group(n, n // 2, n % 2, TAIL if n == FULL else 128))
                for u in range(2):
                    sp.wait_ge(s_st[u], GROUPS // 2 * 16)

            @block.gpsimd
            def _(pool):
                def step(g):
                    P = g.P
                    pool.wait_ge(s_rc, g.n + 1)
                    if from_group(g, 1):
                        pool.wait_ge(s_mt, g.n)
                    pool.tensor_tensor(mean[0:P, :, :], es[g.u][0:P, :, 0:D],
                                       rc[0:P, :].unsqueeze(2).to_broadcast([P, T, D]), ALU.mult).then_inc(s_mean, 1)
                over_groups(pool, step)

            @block.tensor
            def _(pe):
                def first(g):
                    P, W = g.P, T * g.P
                    pe.wait_ge(s_x[g.u], (g.h + 1) * 16)
                    if from_group(g, 1):
                        pe.wait_ge(s_xT, g.n)
                    for c in range(T):
                        last = pe.transpose(banks[:, PX, c * P:(c + 1) * P], xr[g.u][0:P, c, :], ident[0:P, 0:P])
                    last.then_inc(s_xt, 1)
                    pe.wait_ge(s_mean, g.n + 1)
                    if from_group(g, 1):
                        pe.wait_ge(s_mT, g.n)
                    for c in range(T):
                        last = pe.transpose(banks[:, PM, c * P:(c + 1) * P], mean[0:P, c, :], ident[0:P, 0:P])
                    last.then_inc(s_mt, 1)
                    pe.wait_ge(s_xT, g.n + 1)
                    if from_group(g, 1):
                        pe.wait_ge(s_pos, g.n)
                        pe.wait_ge(s_ab, g.n)
                    pe.matmul(banks[:, PH, 0:W], wxT[:, :], xT[:, 0:W], start=True, stop=False)
                    pe.wait_ge(s_mT, g.n + 1)
                    pe.matmul(banks[:, PH, 0:W], weT[:, :], mT[:, 0:W], start=False, stop=True).then_inc(s_h, 1)

                def second(g):
                    P = g.P
                    pe.wait_ge(s_soft, g.n + 1)
                    if from_group(g, 1):
                        pe.wait_ge(s_y, g.n)
                    for c in range(T):
                        last = pe.transpose(banks[0:P, PB, c * 128:(c + 1) * 128], sp_[g.u][:, c * P:(c + 1) * P],
                                            ident[:, :])
                    last.then_inc(s_back, 1)

                def step(g):
                    first(g)
                    if near(g, -1):
                        second(near(g, -1))
                over_groups(pe, step)
                second(near(Group(GROUPS, 0, 0, 0), -1))

            @block.scalar
            def _(act):
                def first(g):
                    W = T * g.P
                    act.wait_ge(s_xt, g.n + 1)
                    if from_group(g, 1):
                        act.wait_ge(s_h, g.n)
                    act.activation(xT[:, 0:W], banks[:, PX, 0:W], ACT.Copy).then_inc(s_xT, 1)

                def mid(g):
                    W = T * g.P
                    act.wait_ge(s_h, g.n + 1)
                    if from_group(g, 1):
                        act.wait_ge(s_ex, g.n)
                    act.activation(ab[:, 0:W], banks[:, PH, 0:W], ACT.Abs, bias=gvec[:, :]).then_inc(s_ab, 1)
                    act.wait_ge(s_ab, g.n + 1)
                    if from_group(g, 1):
                        act.wait_ge(s_lg, g.n)
                    act.activation(ex[:, 0:W], ab[:, 0:W], ACT.Exp, scale=-1.0).then_inc(s_ex, 1)
                    act.wait_ge(s_ex, g.n + 1)
                    if from_group(g, 1):
                        act.wait_ge(s_soft, g.n)
                    act.activation(banks[:, PL, 0:W], ex[:, 0:W], ACT.Ln, bias=ones[:, 0:1]).then_inc(s_lg, 1)

                def step(g):
                    first(g)
                    if near(g, -1):
                        norm_root_exp(act, N, near(g, -1))
                    mid(g)
                over_groups(act, step)
                norm_root_exp(act, N, near(Group(GROUPS, 0, 0, 0), -1))

            @block.vector
            def _(dve):
                def counts(g):
                    P = g.P
                    dve.wait_ge(s_es[g.u], (g.h + 1) * 16)
                    if from_group(g, 1):
                        dve.wait_ge(s_rc, g.n)
                    dve.tensor_scalar(cnt[0:P, :], es[g.u][0:P, :, D], 1.0, None, ALU.max).then_inc(s_cnt, 1)
                    dve.wait_ge(s_cnt, g.n + 1)
                    if from_group(g, 1):
                        dve.wait_ge(s_mean, g.n)
                    dve.reciprocal(rc[0:P, :], cnt[0:P, :]).then_inc(s_rc, 1)

                def first(g):
                    W = T * g.P
                    dve.wait_ge(s_mt, g.n + 1)
                    if from_group(g, 1):
                        dve.wait_ge(s_h, g.n)
                    dve.tensor_copy(mT[:, 0:W], banks[:, PM, 0:W]).then_inc(s_mT, 1)

                def soft(g):
                    W = T * g.P
                    dve.wait_ge(s_ab, g.n + 1)
                    if from_group(g, 1):
                        dve.wait_ge(s_soft, g.n)
                    dve.tensor_scalar(pos[:, 0:W], banks[:, PH, 0:W], gvec[:, 0:1], 0.0, ALU.add, ALU.max)\
                       .then_inc(s_pos, 1)
                    dve.wait_ge(s_pos, g.n + 1)
                    dve.wait_ge(s_lg, g.n + 1)
                    if from_group(g, 2):
                        dve.wait_ge(s_back, g.n - 1)
                    dve.scalar_tensor_tensor(out=sp_[g.u][:, 0:W], in0=pos[:, 0:W], scalar=-math.log(2.0),
                                             in1=banks[:, PL, 0:W], op0=ALU.add, op1=ALU.add).then_inc(s_soft, 1)

                def second(g):
                    P = g.P
                    dve.wait_ge(s_back, g.n + 1)
                    if from_group(g, 1):
                        dve.wait_ge(N.s_out, g.n)
                    dve.tensor_tensor(y[0:P, :, :], tiles(banks[:, PB, :], P), xr[g.u][0:P, :, :], ALU.add)\
                       .then_inc(s_y, 1)
                    dve.wait_ge(s_y, g.n + 1)
                    norm_stats(dve, N, g, y[0:P, :, :])

                def third(g):
                    norm_newton(dve, N, g)
                    if from_group(g, 2):
                        dve.wait_ge(s_st[g.u], g.h * 16)
                    norm_apply(dve, N, g, y[0:g.P, :, :], o[g.u][0:g.P, :, :])

                def step(g):
                    p = near(g, -1)
                    counts(g)
                    first(g)
                    if p:
                        second(p)
                        third(p)
                    soft(g)
                over_groups(dve, step)
                p = near(Group(GROUPS, 0, 0, 0), -1)
                second(p)
                third(p)

        def edges(l, table):
            with ExitStack() as c2:
                sem, pair = semaphores(c2, f"a{l}_")

                isrc = [sb(f"isrc{u}", [128, T], I32) for u in range(2)]
                idst = [sb(f"idst{u}", [128, T], I32) for u in range(2)]
                hs = [sb(f"hs{u}", [128, T, D]) for u in range(2)]
                hd = [sb(f"hd{u}", [128, T, D]) for u in range(2)]
                hsT, hdT, kT, prod = (sb(n, [128, 512]) for n in ("hsT", "hdT", "kT", "prod"))
                clip = sb("clip", [128, T * HEADS])
                vals = sb("vals", [128, T, WA])
                sums = [sb(f"asums{u}", [128, T * WA]) for u in range(2)]
                s_ix, s_it, s_dcol, s_spread, s_same = sem("ix"), sem("it"), sem("dcol"), sem("spread"), sem("same")
                s_gat, s_scat = a_gathered[l], a_scattered[l]
                s_st, s_dt, s_hsT, s_hdT = sem("st"), sem("dt"), sem("hsT"), sem("hdT")
                s_k, s_q, s_v, s_kT, s_prod = sem("k"), sem("q"), sem("v"), sem("kT"), sem("prod")
                s_sc, s_clip, s_w, s_vals = sem("score"), sem("clip"), sem("weight"), sem("vals")
                s_mm, s_sums = sem("summed"), sem("sums")
                s_carry_g, s_carry_s = sem("carry_gather"), sem("carry_scatter")
                block = c2.enter_context(nc.Block())
                PS, PT, PK, PQ, PV, PD = 0, 1, 2, 3, 4, 5
                A = banks[:, 6:8, :]
                SC = banks[:, 7, 512 - T * HEADS:512]

                @block.gpsimd
                def _(pool):
                    def gather(g, c):
                        P = g.P
                        if c == 0:
                            pool.wait_ge(s_ix, 2 * (g.n + 1))
                            if from_group(g, 2):
                                pool.wait_ge(s_dt, g.n - 1)
                            carry_wait(pool, g, 0, s_carry_g)
                        for ix, to in ((isrc, hs), (idst, hd)):
                            pool.indirect_dma_start(to[g.u][0:P, c, :], None, table,
                                                    bass.IndirectOffsetOnAxis(ix[g.u][0:P, c:c + 1], 0))\
                                .then_inc(s_gat[g.u], 16)

                    def scatter(g, c):
                        if c == 0:
                            pool.wait_ge(s_it, g.n + 1)
                            pool.wait_ge(s_sums, g.n + 1)
                            if from_group(g, 1):
                                p = near(g, -1)
                                pool.wait_ge(s_scat[p.u], (p.h + 1) * (16 * T))
                            carry_wait(pool, g, 1, s_carry_s)
                        pool.indirect_dma_start(attn_sum[l], bass.IndirectOffsetOnAxis(tgt[g.u][0:g.P, c:c + 1], 0),
                                                sums[g.u][0:g.P, c * WA:(c + 1) * WA], None, compute_op=ALU.add)\
                            .then_inc(s_scat[g.u], 16)

                    for c in range(T):
                        gather(Group(0, 0, 0, 128), c)

                    def step(g):
                        for c in range(T):
                            if near(g, 1):
                                gather(near(g, 1), c)
                        for c in range(T):
                            if near(g, -1):
                                scatter(near(g, -1), c)
                    over_groups(pool, step)
                    for c in range(T):
                        scatter(near(Group(GROUPS, 0, 0, 0), -1), c)
                    for u in range(2):
                        pool.wait_ge(s_scat[u], GROUPS // 2 * 16 * T)

                @block.vector
                def _(dve):
                    def indices(g):
                        dve.tensor_copy(isrc[g.u][0:g.P, :], srcs[0:g.P, bass.ds(g.n * T, T)]).then_inc(s_ix, 1)
                        dve.tensor_copy(idst[g.u][0:g.P, :], dsts[0:g.P, bass.ds(g.n * T, T)]).then_inc(s_ix, 1)

                    indices(Group(0, 0, 0, 128))
                    indices(Group(1, 0, 1, 128))

                    def step(g):
                        P, W = g.P, T * g.P
                        if from_group(g, 2):
                            dve.wait_ge(s_spread, g.n - 1)
                            dve.wait_ge(s_same, T * (g.n - 1))
                        copy_dst(dve, g, s_dcol)
                        dve.wait_ge(s_spread, g.n + 1)
                        dve.wait_ge(s_dcol, g.n + 1)
                        if from_group(g, 2):
                            dve.wait_ge(s_mm, g.n - 1)
                        build_same(dve, g, banks[:, PD, :], s_same)
                        if from_group(g, 2):
                            dve.wait_ge(s_scat[g.u], g.h * (16 * T))
                        dve.tensor_copy(tgt[g.u][0:P, :], tgts[0:P, bass.ds(g.n * T, T)]).then_inc(s_it, 1)
                        dve.wait_ge(s_gat[g.u], (g.h + 1) * (32 * T))
                        if near(g, 2):
                            indices(near(g, 2))
                        dve.wait_ge(s_dt, g.n + 1)
                        if from_group(g, 1):
                            dve.wait_ge(s_q, g.n)
                        dve.tensor_copy(hdT[:, 0:W], banks[:, PT, 0:W]).then_inc(s_hdT, 1)
                        dve.wait_ge(s_q, g.n + 1)
                        dve.wait_ge(s_kT, g.n + 1)
                        if from_group(g, 1):
                            dve.wait_ge(s_sc, g.n)
                        dve.scalar_tensor_tensor(out=prod[:, 0:W], in0=banks[:, PQ, 0:W], scalar=bq[:, l:l + 1],
                                                 in1=kT[:, 0:W], op0=ALU.add, op1=ALU.mult).then_inc(s_prod, 1)
                        dve.wait_ge(s_sc, g.n + 1)
                        if from_group(g, 1):
                            dve.wait_ge(s_w, g.n)
                        dve.tensor_scalar(clip[0:P, :], SC[0:P, :], -5.0, 5.0, ALU.max, ALU.min).then_inc(s_clip, 1)
                        dve.wait_ge(s_w, g.n + 1)
                        dve.wait_ge(s_v, g.n + 1)
                        weight = vals[0:P, :, D:WA].unsqueeze(3).to_broadcast([P, T, HEADS, DK])
                        dve.tensor_tensor(vals[0:P, :, 0:D].rearrange("p c (h k) -> p c h k", h=HEADS),
                                          banks[0:P, PV, :].rearrange("p (c h k) -> p c h k", c=T, h=HEADS),
                                          weight, ALU.mult).then_inc(s_vals, 1)
                    over_groups(dve, step)

                @block.scalar
                def _(act):
                    def step(g):
                        P, W = g.P, T * g.P
                        act.wait_ge(s_st, g.n + 1)
                        if from_group(g, 1):
                            act.wait_ge(s_v, g.n)
                        act.activation(hsT[:, 0:W], banks[:, PS, 0:W], ACT.Copy).then_inc(s_hsT, 1)
                        act.wait_ge(s_k, g.n + 1)
                        if from_group(g, 1):
                            act.wait_ge(s_prod, g.n)
                        act.activation(kT[:, 0:W], banks[:, PK, 0:W], ACT.Identity, bias=bk[:, l:l + 1])\
                           .then_inc(s_kT, 1)
                        act.wait_ge(s_clip, g.n + 1)
                        if from_group(g, 1):
                            act.wait_ge(s_mm, g.n)
                        act.activation(vals[0:P, :, D:WA], clip[0:P, :].rearrange("p (c h) -> p c h", c=T), ACT.Exp)\
                           .then_inc(s_w, 1)
                        act.wait_ge(s_mm, g.n + 1)
                        if from_group(g, 2):
                            act.wait_ge(s_scat[g.u], g.h * (16 * T))
                        act.activation(sums[g.u][0:P, :].rearrange("p (k f) -> p k f", k=2), A[0:P, :, 0:2 * WA],
                                       ACT.Copy).then_inc(s_sums, 1)
                    over_groups(act, step)

                @block.tensor
                def _(pe):
                    def step(g):
                        P, W = g.P, T * g.P
                        pe.wait_ge(s_dcol, g.n + 1)
                        if from_group(g, 1):
                            pe.wait_ge(s_same, T * g.n)
                        spread_dst(pe, g, banks[:, PD, :], s_spread)
                        pe.wait_ge(s_gat[g.u], (g.h + 1) * (32 * T))
                        if from_group(g, 1):
                            pe.wait_ge(s_hsT, g.n)
                            pe.wait_ge(s_hdT, g.n)
                        for bank, h, done in ((PS, hs, s_st), (PT, hd, s_dt)):
                            for c in range(T):
                                last = pe.transpose(banks[:, bank, c * P:(c + 1) * P], h[g.u][0:P, c, :],
                                                    ident[0:P, 0:P])
                            last.then_inc(done, 1)
                        pe.wait_ge(s_hsT, g.n + 1)
                        if from_group(g, 1):
                            pe.wait_ge(s_kT, g.n)
                        pe.matmul(banks[:, PK, 0:W], wk[:, l, :], hsT[:, 0:W], start=True, stop=True).then_inc(s_k, 1)
                        pe.wait_ge(s_hdT, g.n + 1)
                        if from_group(g, 1):
                            pe.wait_ge(s_prod, g.n)
                        pe.matmul(banks[:, PQ, 0:W], wq[:, l, :], hdT[:, 0:W], start=True, stop=True).then_inc(s_q, 1)
                        if from_group(g, 1):
                            pe.wait_ge(s_vals, g.n)
                        for c in range(T):
                            to = banks[0:P, PV, c * 128:(c + 1) * 128]
                            pe.matmul(to, hsT[:, c * P:(c + 1) * P], wv[:, l, :], start=True, stop=False)
                            last = pe.matmul(to, ones[0:1, 0:P], bv[:, l, :], start=False, stop=True)
                        last.then_inc(s_v, 1)
                        pe.wait_ge(s_prod, g.n + 1)
                        if from_group(g, 1):
                            pe.wait_ge(s_clip, g.n)
                            pe.wait_ge(s_sums, g.n)
                        for c in range(T):
                            last = pe.matmul(SC[0:P, c * HEADS:(c + 1) * HEADS], prod[:, c * P:(c + 1) * P],
                                             heads[:, :], start=True, stop=True)
                        last.then_inc(s_sc, 1)
                        pe.wait_ge(s_vals, g.n + 1)
                        pe.wait_ge(s_same, T * (g.n + 1))
                        pe.wait_ge(s_clip, g.n + 1)
                        sum_same(pe, g, vals, WA, A, s_mm)
                    over_groups(pe, step)

        def nodes(l, table, to_dram, last_layer):
            with ExitStack() as c2:
                sem, pair = semaphores(c2, f"n{l}_")

                ag = [sb(f"ag{u}", [128, T, WA]) for u in range(2)]
                hr = [sb(f"hr{u}", [128, T, D]) for u in range(2)]
                xs = [sb(f"xs{u}", [128, T, D]) for u in range(2)]
                z, rz = sb("z", [128, T, HEADS]), sb("rz", [128, T, HEADS])
                at, hb = (sb(n, [128, T, D]) for n in ("at", "hb"))
                atT = sb("atT", [128, 512])
                y, xh = (sb(n, [128, T, D]) for n in ("y", "xh"))
                h1T, r0, r1, y2T = (sb(n, [128, 512]) for n in ("h1T", "r0", "r1", "y2T"))
                xo, sg, res = (sb(n, [128, T, D]) for n in ("xo", "sg", "res"))
                o = [sb(f"o{u}", [128, T, D]) for u in range(2)]
                N1, N2 = Norm(sem, f"n{l}a", 1), Norm(sem, f"n{l}b", 2)
                N3 = Norm(sem, f"n{l}c", 3) if last_layer else None
                s_ag, s_hr, s_xs, s_st = pair("ag"), pair("hr"), pair("xs"), pair("stored")
                s_z, s_rz, s_at, s_hb = sem("z"), sem("rz"), sem("at"), sem("hb")
                s_att, s_atT, s_wo, s_y = sem("att"), sem("atT"), sem("wo"), sem("y")
                s_xt, s_h1T, s_w1, s_r0, s_r1 = sem("xt"), sem("h1T"), sem("w1"), sem("r0"), sem("r1")
                s_w2, s_y2T, s_back, s_sg, s_o, s_res = (sem(n) for n in ("w2", "y2T", "back", "sg", "o", "res"))
                block = c2.enter_context(nc.Block())
                PA, PW, PX, PR0, PR1, PF, PB = range(7)
                out_ready = N3.s_out if last_layer else s_o
                end = Group(GROUPS, 0, 0, 0)
                tail1, tail2 = near(end, -1), near(end, -2)

                @block.sync
                def _(sp):
                    def store(g):
                        sp.wait_ge(out_ready, g.n + 1)
                        sp.dma_start(rows_of(to_dram, g, D), o[g.u][0:g.P, :, :].rearrange("p c f -> p (c f)"))\
                          .then_inc(s_st[g.u], 16)

                    def step(g):
                        if from_group(g, 2):
                            sp.wait_ge(s_at, g.n - 1)
                        sp.dma_start(ag[g.u][0:g.P, :, :],
                                     rows_of(attn_sum[l], g, WA).rearrange("p (c f) -> p c f", c=T))\
                          .then_inc(s_ag[g.u], 16)
                        if from_group(g, 2):
                            sp.wait_ge(s_hb, g.n - 1)
                        sp.dma_start(hr[g.u][0:g.P, :, :], rows_of(table, g, D).rearrange("p (c f) -> p c f", c=T))\
                          .then_inc(s_hr[g.u], 16)
                        if last_layer:
                            if from_group(g, 2):
                                sp.wait_ge(s_res, g.n - 1)
                            sp.dma_start(xs[g.u][0:g.P, :, :], rows_of(x1, g, D).rearrange("p (c f) -> p c f", c=T))\
                              .then_inc(s_xs[g.u], 16)
                        if near(g, -2):
                            store(near(g, -2))
                    over_groups(sp, step)
                    store(tail2)
                    store(tail1)
                    for u in range(2):
                        sp.wait_ge(s_st[u], GROUPS // 2 * 16)

                @block.gpsimd
                def _(pool):
                    def first(g):
                        P = g.P
                        pool.wait_ge(s_hr[g.u], (g.h + 1) * 16)
                        if from_group(g, 1):
                            pool.wait_ge(s_y, g.n)
                        pool.tensor_tensor(hb[0:P, :, :], hr[g.u][0:P, :, :],
                                           bo[0:P, l, :].unsqueeze(1).to_broadcast([P, T, D]), ALU.add)\
                            .then_inc(s_hb, 1)
                        pool.wait_ge(s_rz, g.n + 1)
                        if from_group(g, 1):
                            pool.wait_ge(s_att, g.n)
                        pool.tensor_tensor(at[0:P, :, :].rearrange("p c (h k) -> p c h k", h=HEADS),
                                           ag[g.u][0:P, :, 0:D].rearrange("p c (h k) -> p c h k", h=HEADS),
                                           rz[0:P, :, :].unsqueeze(3).to_broadcast([P, T, HEADS, DK]), ALU.mult)\
                            .then_inc(s_at, 1)

                    def second(g):
                        P = g.P
                        pool.wait_ge(N2.s_out, g.n + 1)
                        if from_group(g, 1):
                            pool.wait_ge(s_o, g.n)
                        pool.tensor_tensor(sg[0:P, :, :], xo[0:P, :, :],
                                           g2[0:P, l, :].unsqueeze(1).to_broadcast([P, T, D]), ALU.mult)\
                            .then_inc(s_sg, 1)
                        pool.wait_ge(s_sg, g.n + 1)
                        to = res if last_layer else o[g.u]
                        if last_layer:
                            if from_group(g, 1):
                                pool.wait_ge(N3.s_out, g.n)
                        elif from_group(g, 2):
                            pool.wait_ge(s_st[g.u], g.h * 16)
                        pool.tensor_tensor(to[0:P, :, :], sg[0:P, :, :],
                                           be2[0:P, l, :].unsqueeze(1).to_broadcast([P, T, D]), ALU.add)\
                            .then_inc(s_o, 1)
                        if last_layer:
                            pool.wait_ge(s_o, g.n + 1)
                            pool.wait_ge(s_xs[g.u], (g.h + 1) * 16)
                            pool.tensor_tensor(res[0:P, :, :], res[0:P, :, :], xs[g.u][0:P, :, :], ALU.add)\
                                .then_inc(s_res, 1)

                    def step(g):
                        first(g)
                        if near(g, -2):
                            second(near(g, -2))
                    over_groups(pool, step)
                    second(tail2)
                    second(tail1)

                @block.tensor
                def _(pe):
                    def attn(g):
                        P = g.P
                        pe.wait_ge(s_at, g.n + 1)
                        if from_group(g, 1):
                            pe.wait_ge(s_atT, g.n)
                        for c in range(T):
                            last = pe.transpose(banks[:, PA, c * P:(c + 1) * P], at[0:P, c, :], ident[0:P, 0:P])
                        last.then_inc(s_att, 1)

                    def project(g):
                        P = g.P
                        pe.wait_ge(s_atT, g.n + 1)
                        if from_group(g, 1):
                            pe.wait_ge(s_y, g.n)
                        for c in range(T):
                            last = pe.matmul(banks[0:P, PW, c * 128:(c + 1) * 128], atT[:, c * P:(c + 1) * P],
                                             wo[:, l, :], start=True, stop=True)
                        last.then_inc(s_wo, 1)

                    def turn(g):
                        P = g.P
                        pe.wait_ge(N1.s_out, g.n + 1)
                        if from_group(g, 1):
                            pe.wait_ge(s_h1T, g.n)
                        for c in range(T):
                            last = pe.transpose(banks[:, PX, c * P:(c + 1) * P], xh[0:P, c, :], ident[0:P, 0:P])
                        last.then_inc(s_xt, 1)

                    def up(g):
                        W = T * g.P
                        pe.wait_ge(s_h1T, g.n + 1)
                        for k, (bank, used) in enumerate(((PR0, s_r0), (PR1, s_r1))):
                            if from_group(g, 1):
                                pe.wait_ge(used, g.n)
                            pe.matmul(banks[:, bank, 0:W], w1[:, l, 128 * k:128 * (k + 1)], h1T[:, 0:W],
                                      start=True, stop=True).then_inc(s_w1, 1)

                    def down(g):
                        W = T * g.P
                        pe.wait_ge(s_r0, g.n + 1)
                        if from_group(g, 1):
                            pe.wait_ge(s_y2T, g.n)
                        pe.matmul(banks[:, PF, 0:W], w2[:, l, 0, :], r0[:, 0:W], start=True, stop=False)
                        pe.wait_ge(s_r1, g.n + 1)
                        pe.matmul(banks[:, PF, 0:W], w2[:, l, 1, :], r1[:, 0:W], start=False, stop=True)\
                          .then_inc(s_w2, 1)

                    def back(g):
                        P = g.P
                        pe.wait_ge(s_y2T, g.n + 1)
                        if from_group(g, 1):
                            pe.wait_ge(N2.s_out, g.n)
                        for c in range(T):
                            last = pe.transpose(banks[0:P, PB, c * 128:(c + 1) * 128], y2T[:, c * P:(c + 1) * P],
                                                ident[:, :])
                        last.then_inc(s_back, 1)

                    def step(g):
                        p = near(g, -1)
                        attn(g)
                        if p:
                            turn(p)
                        project(g)
                        if p:
                            up(p)
                            down(p)
                            back(p)
                    over_groups(pe, step)
                    for part in (turn, up, down, back):
                        part(tail1)

                @block.scalar
                def _(act):
                    def attn(g):
                        W = T * g.P
                        act.wait_ge(s_att, g.n + 1)
                        if from_group(g, 1):
                            act.wait_ge(s_wo, g.n)
                        act.activation(atT[:, 0:W], banks[:, PA, 0:W], ACT.Copy).then_inc(s_atT, 1)

                    def scale(g):
                        W = T * g.P
                        act.wait_ge(s_xt, g.n + 1)
                        if from_group(g, 1):
                            act.wait_ge(s_y2T, g.n)
                        act.activation(h1T[:, 0:W], banks[:, PX, 0:W], ACT.Identity, bias=be1[:, l:l + 1],
                                       scale=g1[:, l:l + 1]).then_inc(s_h1T, 1)

                    def relu(g):
                        W = T * g.P
                        act.wait_ge(s_w1, 2 * g.n + 1)
                        if from_group(g, 1):
                            act.wait_ge(s_w2, g.n)
                        act.activation(r0[:, 0:W], banks[:, PR0, 0:W], ACT.Relu, bias=b1[:, 2 * l:2 * l + 1])\
                           .then_inc(s_r0, 1)

                    def step(g):
                        p, q = near(g, -1), near(g, -2)
                        attn(g)
                        if p:
                            scale(p)
                            relu(p)
                        norm_root(act, N1, g)
                        if p:
                            norm_root(act, N2, p)
                        if last_layer and q:
                            norm_root(act, N3, q)
                    over_groups(act, step)
                    scale(tail1)
                    relu(tail1)
                    norm_root(act, N2, tail1)
                    if last_layer:
                        norm_root(act, N3, tail2)
                        norm_root(act, N3, tail1)

                @block.vector
                def _(dve):
                    def recip_z(g):
                        P = g.P
                        dve.wait_ge(s_ag[g.u], (g.h + 1) * 16)
                        if from_group(g, 1):
                            dve.wait_ge(s_rz, g.n)
                        dve.tensor_scalar(z[0:P, :, :], ag[g.u][0:P, :, D:WA], 1e-6, None, ALU.add).then_inc(s_z, 1)
                        dve.wait_ge(s_z, g.n + 1)
                        if from_group(g, 1):
                            dve.wait_ge(s_at, g.n)
                        dve.reciprocal(rz[0:P, :, :], z[0:P, :, :]).then_inc(s_rz, 1)

                    def stats1(g):
                        P = g.P
                        dve.wait_ge(s_wo, g.n + 1)
                        dve.wait_ge(s_hb, g.n + 1)
                        if from_group(g, 1):
                            dve.wait_ge(N1.s_out, g.n)
                        dve.tensor_tensor(y[0:P, :, :], tiles(banks[:, PW, :], P), hb[0:P, :, :], ALU.add)\
                           .then_inc(s_y, 1)
                        dve.wait_ge(s_y, g.n + 1)
                        norm_stats(dve, N1, g, y[0:P, :, :])

                    def apply1(g):
                        norm_recip(dve, N1, g)
                        if from_group(g, 1):
                            dve.wait_ge(s_xt, g.n)
                        norm_apply(dve, N1, g, y[0:g.P, :, :], xh[0:g.P, :, :])

                    def relu(g):
                        W = T * g.P
                        dve.wait_ge(s_w1, 2 * g.n + 2)
                        if from_group(g, 1):
                            dve.wait_ge(s_w2, g.n)
                        dve.tensor_scalar(r1[:, 0:W], banks[:, PR1, 0:W], b1[:, 2 * l + 1:2 * l + 2], 0.0,
                                          ALU.add, ALU.max).then_inc(s_r1, 1)

                    def residual(g):
                        W = T * g.P
                        dve.wait_ge(s_w2, g.n + 1)
                        dve.wait_ge(s_h1T, g.n + 1)
                        if from_group(g, 1):
                            dve.wait_ge(s_back, g.n)
                        dve.scalar_tensor_tensor(out=y2T[:, 0:W], in0=banks[:, PF, 0:W], scalar=b2[:, l:l + 1],
                                                 in1=h1T[:, 0:W], op0=ALU.add, op1=ALU.add).then_inc(s_y2T, 1)

                    def stats2(g):
                        dve.wait_ge(s_back, g.n + 1)
                        norm_stats(dve, N2, g, tiles(banks[:, PB, :], g.P))

                    def apply2(g):
                        norm_recip(dve, N2, g)
                        if from_group(g, 1):
                            dve.wait_ge(s_sg, g.n)
                        norm_apply(dve, N2, g, tiles(banks[:, PB, :], g.P), xo[0:g.P, :, :])

                    def stats3(g):
                        dve.wait_ge(s_res, g.n + 1)
                        norm_stats(dve, N3, g, res[0:g.P, :, :])

                    def apply3(g):
                        norm_recip(dve, N3, g)
                        if from_group(g, 2):
                            dve.wait_ge(s_st[g.u], g.h * 16)
                        norm_apply(dve, N3, g, res[0:g.P, :, :], o[g.u][0:g.P, :, :])

                    def step(g):
                        p, q = near(g, -1), near(g, -2)
                        recip_z(g)
                        if p:
                            relu(p)
                        stats1(g)
                        if p:
                            residual(p)
                        apply1(g)
                        if p:
                            stats2(p)
                        if last_layer and q:
                            stats3(q)
                        if p:
                            apply2(p)
                        if last_layer and q:
                            apply3(q)
                    over_groups(dve, step)
                    relu(tail1)
                    residual(tail1)
                    stats2(tail1)
                    if last_layer:
                        stats3(tail2)
                    apply2(tail1)
                    if last_layer:
                        apply3(tail2)
                        stats3(tail1)
                        apply3(tail1)

        edges(0, x1)
        nodes(0, x1, h1, False)
        edges(1, h1)
        nodes(1, h1, out, True)


_INS = {"x": "x", "src": "src", "dst": "dst", "edge_attr_128": "edge", "L0_gnn_global_feats": "glob", "L0_gnn_W": "W"}
_INS.update({f"L1_gnn_{n}": n for n in ("Wq", "bq", "Wk", "bk", "Wv", "bv", "Wo", "bo", "W1", "b1", "W2", "b2",
                                        "ln1_g", "ln1_b", "ln2_g", "ln2_b")})


def kernel(**inputs):
    import numpy as _np
    import concourse.bacc as _bacc
    from concourse import mybir as _mybir
    from concourse.bass_utils import run_bass_kernel_spmd as _run

    nc = _bacc.Bacc("TRN2", target_bir_lowering=False, num_devices=1)
    arrays, args = {}, {}
    for name, short in _INS.items():
        v = _np.ascontiguousarray(inputs[name])
        arrays[f"in_{name}"] = v
        args[short] = nc.dram_tensor(f"in_{name}", v.shape, _mybir.dt.from_np(v.dtype), kind="ExternalInput").ap()
    out = nc.dram_tensor("out_0", (NODES, D), F32, kind="ExternalOutput").ap()
    program(nc, args, out)
    r = _run(nc, [arrays], core_ids=[0])
    return r.results[0]["out_0"]
```

```python
from collections import namedtuple
from contextlib import ExitStack
import math

import concourse.bass as bass
from concourse import mybir

F32 = mybir.dt.float32
I32 = mybir.dt.int32
ALU = mybir.AluOpType
ACT = mybir.ActivationFunctionType

NODES = 50000
D = 128
HEADS = 8
DK = D // HEADS
LAYERS = 2
T = 4
ROWS = 128 * T
FULL = NODES // ROWS
TAIL = (NODES - FULL * ROWS) // T
GROUPS = FULL + 1
PAD = (GROUPS + 1) * ROWS
DUMP = GROUPS * ROWS
WM = D + 1
WA = D + HEADS
EPS = 1e-5

assert NODES == FULL * ROWS + TAIL * T and GROUPS % 2 == 0

Group = namedtuple("Group", "n h u P")


def near(g, d):
    k = g.u + d
    n = g.n + d
    if isinstance(n, int):
        if n < 0 or n >= GROUPS:
            return None
        return Group(n, n // 2, n % 2, TAIL if n == FULL else 128)
    return Group(n, g.h + k // 2, k % 2, 128)


def from_group(g, k):
    return not isinstance(g.n, int) or g.n >= k


FIRST, LAST = 10, (GROUPS - 4) // 2 * 2


def over_groups(eng, step, lag=0):
    def peeled(n):
        step(Group(n, n // 2, n % 2, TAIL if n == FULL else 128))

    for n in range(FIRST):
        peeled(n)
    with eng.Fori(FIRST // 2, LAST // 2) as h:
        for u in range(2):
            step(Group(h * 2 + u, h, u, 128))
    for n in range(LAST, GROUPS + lag):
        peeled(n)


def rows_of(dram, g, width):
    if isinstance(g.n, int) and g.n == FULL:
        part = dram[FULL * ROWS:NODES, :]
        return part.rearrange("(p c) f -> p (c f)", c=T)
    full = dram[0:FULL * ROWS, :].rearrange("(g p c) f -> g p (c f)", p=128, c=T)
    return full[g.n, :, :]


def tiles(t, P):
    return t[0:P, :].rearrange("p (c f) -> p c f", c=T)


def program(nc, a, out):
    with ExitStack() as ctx:
        buffers = {}

        def sb(name, shape, dt=F32):
            if name not in buffers:
                buffers[name] = ctx.enter_context(nc.sbuf_tensor(name, shape, dt))
            return buffers[name]

        def gpsimd_pair(name):
            return [ctx.enter_context(nc.semaphore(f"{name}{u}")) for u in range(2)]

        e_scattered = gpsimd_pair("e_scattered")
        a_gathered = [gpsimd_pair(f"a{l}_gathered") for l in range(LAYERS)]
        a_scattered = [gpsimd_pair(f"a{l}_scattered") for l in range(LAYERS)]
        nc.all_engine_barrier()
        first_num = nc.alloc_semaphore(name="first")
        nc.release_semaphore(first_num)

        def semaphores(phase, prefix=""):
            made = []

            def sem(name):
                made.append(phase.enter_context(nc.semaphore(prefix + name, num=first_num.num + len(made))))
                return made[-1]

            def pair(name):
                return [sem(f"{name}0"), sem(f"{name}1")]

            phase.callback(lambda: nc.all_engine_barrier(sems_to_clear=range(made[0].num, made[-1].num + 1)))
            return sem, pair

        def dram(name, rows, width):
            return nc.dram_tensor(name, (rows, width), F32, kind="Internal").ap()

        edge_sum = dram("edge_sum", PAD, WM)
        attn_sum = [dram(f"attn_sum{l}", PAD, WA) for l in range(LAYERS)]
        x1 = dram("x1", NODES, D)
        h1 = dram("h1", NODES, D)

        banks = ctx.enter_context(nc.psum_tensor("banks", [128, 8, 512], F32))

        ident = sb("ident", [128, 128])
        early = sb("early", [128, T, 128])
        zeros = sb("zeros", [128, T * WA])
        ones = sb("ones", [128, 128])
        heads = sb("heads", [128, HEADS])
        dumprow = sb("dumprow", [128, T])
        eps = sb("eps", [128, 1])
        w0 = sb("w0", [128, 320])
        wxT = sb("wxT", [128, 128])
        weT = sb("weT", [128, 128])
        wgT = sb("wgT", [64, 128])
        glob = sb("glob", [64, 1])
        gvec = sb("gvec", [128, 1])
        wq, wk, wv, wo = (sb(f"w{n}", [128, LAYERS, 128]) for n in "qkvo")
        w1 = sb("w1", [128, LAYERS, 256])
        w2 = sb("w2", [128, LAYERS, 2, 128])
        bq, bk, b2, g1, be1 = (sb(n, [128, LAYERS]) for n in ("bq", "bk", "b2", "g1", "be1"))
        b1 = sb("b1", [128, LAYERS * 2])
        bv = sb("bv", [1, LAYERS, 128])
        bo, g2, be2 = (sb(n, [128, LAYERS, 128]) for n in ("bo", "g2", "be2"))
        srcs, dsts, tgts = (sb(n, [128, GROUPS * T], I32) for n in ("srcs", "dsts", "tgts"))
        dstf = sb("dstf", [128, GROUPS * T])

        with ExitStack() as c2:
            sem, pair = semaphores(c2)
            s_const = sem("setup_const")
            s_w0 = sem("setup_w0")
            s_idx = sem("setup_idx")
            s_ld = sem("setup_loads")
            s_zero = sem("setup_zero")
            s_clear = sem("setup_clear")
            s_t = sem("setup_wT")
            s_tc = sem("setup_wT_copied")
            s_gv = sem("setup_gvec")
            s_masks = sem("setup_masks")
            s_done = sem("setup_dve")
            loads = [
                (wq[:, :, :], a["Wq"].rearrange("l k m -> k l m")), (wk[:, :, :], a["Wk"].rearrange("l k m -> k l m")),
                (wv[:, :, :], a["Wv"].rearrange("l k m -> k l m")), (wo[:, :, :], a["Wo"].rearrange("l k m -> k l m")),
                (w1[:, :, :], a["W1"].rearrange("l k m -> k l m")),
                (bv[:, :, :], a["bv"].rearrange("(a l) d -> a l d", a=1)),
            ]
            loads += [(w2[:, l, :, :], a["W2"][l, :, :].rearrange("(c k) m -> k c m", k=128)) for l in range(LAYERS)]
            loads += [(t[:, l:l + 1], a[n][l, :].rearrange("(d a) -> d a", a=1)) for t, n in
                      ((bq, "bq"), (bk, "bk"), (b2, "b2"), (g1, "ln1_g"), (be1, "ln1_b")) for l in range(LAYERS)]
            loads += [(b1[:, 2 * l + k:2 * l + k + 1], a["b1"][l, 128 * k:128 * (k + 1)].rearrange("(d a) -> d a", a=1))
                      for l in range(LAYERS) for k in range(2)]
            loads += [(t[:, l, :], a[n][l, :].partition_broadcast(128)) for t, n in
                      ((bo, "bo"), (g2, "ln2_g"), (be2, "ln2_b")) for l in range(LAYERS)]
            block = c2.enter_context(nc.Block())

            @block.sync
            def _(sp):
                sp.dma_start(w0[:, :], a["W"]).then_inc(s_w0, 16)
                sp.dma_start(glob[:, :], a["glob"][0, :].rearrange("(k a) -> k a", a=1)).then_inc(s_w0, 16)
                sp.wait_ge(s_clear, 3)
                for t, n in ((dsts, "dst"), (srcs, "src")):
                    full = a[n][0:FULL * ROWS].rearrange("(g p c) -> p g c", p=128, c=T)
                    sp.dma_start(t[:, 0:FULL * T].rearrange("p (g c) -> p g c", c=T), full).then_inc(s_idx, 16)
                    sp.dma_start(t[0:TAIL, FULL * T:], a[n][FULL * ROWS:NODES].rearrange("(p c) -> p c", c=T))\
                      .then_inc(s_idx, 16)
                for to, fr in loads:
                    sp.dma_start(to, fr).then_inc(s_ld, 16)
                sp.wait_ge(s_ld, 16 * len(loads))
                sp.wait_ge(s_zero, 16 * (GROUPS + 1))

            @block.scalar
            def _(act):
                act.wait_ge(s_clear, 1)
                for g in range(GROUPS + 1):
                    act.dma_start(edge_sum[g * ROWS:(g + 1) * ROWS, :].rearrange("(p c) f -> p (c f)", c=T),
                                  zeros[:, 0:T * WM]).then_inc(s_zero, 16)

            @block.gpsimd
            def _(pool):
                pool.memset(ident[:, :], 0.0).then_inc(s_const, 1)
                pool.memset(early[:, :, :], 1.0).then_inc(s_const, 1)
                pool.memset(heads[:, :], DK ** -0.5).then_inc(s_const, 1)
                pool.memset(ones[:, :], 1.0).then_inc(s_const, 1)
                pool.memset(eps[:, :], EPS).then_inc(s_const, 1)
                pool.iota(dumprow[:, :], pattern=[[128, T]], base=DUMP, channel_multiplier=1,
                          allow_small_or_imprecise_dtypes=True).then_inc(s_const, 1)
                pool.wait_ge(s_const, 6)
                pool.affine_select(out=ident[:, :], in_=ident[:, :], compare_op=ALU.not_equal, fill=1.0, base=0,
                                   pattern=[[-1, 128]], channel_multiplier=1).then_inc(s_masks, 1)
                pool.affine_select(out=early[:, 3, :], in_=early[:, 3, :], compare_op=ALU.is_gt, fill=0.0, base=0,
                                   pattern=[[-1, 128]], channel_multiplier=1).then_inc(s_masks, 1)
                pool.affine_select(out=heads[:, :], in_=heads[:, :], compare_op=ALU.is_ge, fill=0.0, base=0,
                                   pattern=[[-DK, HEADS]], channel_multiplier=1).then_inc(s_masks, 1)
                pool.wait_ge(s_masks, 3)
                pool.affine_select(out=heads[:, :], in_=heads[:, :], compare_op=ALU.is_ge, fill=0.0, base=DK - 1,
                                   pattern=[[DK, HEADS]], channel_multiplier=-1).then_inc(s_masks, 1)

            @block.vector
            def _(dve):
                dve.memset(zeros[:, :], 0.0).then_inc(s_clear, 1)
                dve.memset(srcs[:, :], 0.0).then_inc(s_clear, 1)
                dve.memset(dsts[:, :], 0.0).then_inc(s_clear, 1)
                dve.memset(tgts[:, :], 0.0).then_inc(s_done, 1)
                for k, (t, n) in enumerate(((wxT, 128), (weT, 128), (wgT, 64))):
                    dve.wait_ge(s_t, k + 1)
                    dve.tensor_copy(t[:, :], banks[0:n, k, 0:128]).then_inc(s_tc, 1)
                dve.wait_ge(s_gv, 1)
                dve.tensor_copy(gvec[:, :], banks[:, 3, 0:1]).then_inc(s_done, 1)
                dve.wait_ge(s_idx, 64)
                dve.tensor_copy(dstf[:, :], dsts[:, :]).then_inc(s_done, 1)

            @block.tensor
            def _(pe):
                pe.wait_ge(s_w0, 32)
                pe.wait_ge(s_masks, 1)
                for k, n in enumerate((128, 128, 64)):
                    pe.transpose(banks[0:n, k, 0:128], w0[:, 128 * k:128 * k + n], ident[:, :]).then_inc(s_t, 1)
                pe.wait_ge(s_tc, 3)
                pe.matmul(banks[:, 3, 0:1], wgT[:, :], glob[:, :], start=True, stop=True).then_inc(s_gv, 1)

        nudge = sb("nudge", [128, 8])

        def carry_wait(eng, g, col, used):
            if from_group(g, 1):
                eng.wait_ge(used, g.n)
            eng.tensor_tensor(nudge[:, col:col + 1], ones[:, 0:1], ones[:, 0:1], ALU.mult).then_inc(used, 1)

        dcol = [sb(f"dcol{u}", [128, T]) for u in range(2)]
        same = [sb(f"same{u}", [128, T, T, 128]) for u in range(2)]
        tgt = [sb(f"tgt{u}", [128, T], I32) for u in range(2)]

        def copy_dst(dve, g, ready):
            dve.tensor_copy(dcol[g.u][0:g.P, :], dstf[0:g.P, bass.ds(g.n * T, T)]).then_inc(ready, 1)

        def spread_dst(pe, g, bank, ready):
            P = g.P
            for c in range(T):
                last = pe.transpose(bank[0:P, c * 128:c * 128 + P], dcol[g.u][0:P, c:c + 1].to_broadcast([P, P]),
                                    ident[0:P, 0:P])
            last.then_inc(ready, 1)

        def build_same(dve, g, bank, ready):
            P = g.P
            seen = tiles(bank, P)[:, :, 0:P]
            for c in range(T):
                dve.tensor_scalar(same[g.u][0:P, c, :, 0:P], seen, dcol[g.u][0:P, c:c + 1], None, ALU.is_equal)\
                   .then_inc(ready, 1)

        def sum_same(pe, g, rows, width, sums, ready):
            P = g.P
            for b in range(T):
                to = sums[0:P, b // 2, (b % 2) * width:(b % 2 + 1) * width]
                for c in range(T):
                    last = pe.matmul(to, same[g.u][0:P, c, b, 0:P], rows[0:P, c, 0:width],
                                     start=(c == 0), stop=(c == T - 1))
            last.then_inc(ready, 1)

        with ExitStack() as c2:
            sem, pair = semaphores(c2)
            feat = [sb(f"feat{u}", [128, T, WM]) for u in range(2)]
            sums = [sb(f"esums{u}", [128, T * WM]) for u in range(2)]
            junk = sb("junk", [128, T, 128])
            before = [sb(f"before{u}", [128, T]) for u in range(2)]
            away = sb("away", [128, T])
            shift = sb("shift", [128, T])
            s_one = sem("e_ones")
            s_feat = pair("e_feat")
            s_dcol = sem("e_dcol")
            s_spread = sem("e_spread")
            s_same = sem("e_same")
            s_before = sem("e_before")
            s_away = sem("e_away")
            s_shift = sem("e_shift")
            s_tgt = sem("e_tgt")
            s_keep = sem("e_keep")
            s_mm = sem("e_summed")
            s_sums = sem("e_sums")
            s_scat = e_scattered
            s_zero = pair("e_zeroed")
            s_carry = sem("e_carry")
            block = c2.enter_context(nc.Block())

            @block.sync
            def _(sp):
                sp.wait_ge(s_one, 2)

                def step(g):
                    if from_group(g, 2):
                        sp.wait_ge(s_mm, g.n - 1)
                    src = rows_of(a["edge"], g, D).rearrange("p (c f) -> p c f", c=T)
                    sp.dma_start(feat[g.u][0:g.P, :, 0:D], src).then_inc(s_feat[g.u], 16)
                over_groups(sp, step)

            @block.scalar
            def _(act):
                def zero(g):
                    for l in range(LAYERS):
                        part = attn_sum[l].rearrange("(g p c) f -> g p (c f)", p=128, c=T)[g.n, :, :]
                        act.dma_start(part, zeros[:, :]).then_inc(s_zero[g.u], 16)

                def step(g):
                    zero(g)
                    act.wait_ge(s_mm, g.n + 1)
                    if from_group(g, 2):
                        act.wait_ge(s_scat[g.u], g.h * (16 * T))
                    act.activation(sums[g.u][0:g.P, :].rearrange("p (k f) -> p k f", k=2),
                                   banks[0:g.P, 2 + 2 * g.u:4 + 2 * g.u, 0:2 * WM], ACT.Copy).then_inc(s_sums, 1)
                over_groups(act, step)
                zero(Group(GROUPS, GROUPS // 2, 0, 128))
                act.wait_ge(s_zero[0], 32 * (GROUPS // 2 + 1))
                act.wait_ge(s_zero[1], 32 * (GROUPS // 2))

            @block.gpsimd
            def _(pool):
                def step(g):
                    pool.wait_ge(s_tgt, g.n + 1)
                    pool.wait_ge(s_sums, g.n + 1)
                    if from_group(g, 1):
                        p = near(g, -1)
                        pool.wait_ge(s_scat[p.u], (p.h + 1) * (16 * T))
                    carry_wait(pool, g, 0, s_carry)
                    for c in range(T):
                        pool.indirect_dma_start(edge_sum, bass.IndirectOffsetOnAxis(tgt[g.u][0:g.P, c:c + 1], 0),
                                                sums[g.u][0:g.P, c * WM:(c + 1) * WM], None, compute_op=ALU.add)\
                            .then_inc(s_scat[g.u], 16)
                over_groups(pool, step)
                pool.wait_ge(s_scat[0], GROUPS // 2 * 16 * T)
                pool.wait_ge(s_scat[1], GROUPS // 2 * 16 * T)

            @block.vector
            def _(dve):
                for u in range(2):
                    dve.memset(feat[u][:, :, D:WM], 1.0).then_inc(s_one, 1)
                copy_dst(dve, Group(0, 0, 0, 128), s_dcol)

                def step(g):
                    nxt = near(g, 1)
                    if nxt:
                        if from_group(g, 1):
                            dve.wait_ge(s_keep, g.n)
                            dve.wait_ge(s_spread, g.n)
                        copy_dst(dve, nxt, s_dcol)
                    dve.wait_ge(s_spread, g.n + 1)
                    dve.wait_ge(s_dcol, g.n + 1)
                    if from_group(g, 2):
                        dve.wait_ge(s_mm, g.n - 1)
                    bank = banks[:, g.u, :]
                    build_same(dve, g, bank, s_same)
                    P = g.P
                    for c in range(T):
                        if c or from_group(g, 1):
                            dve.wait_ge(s_before, g.n * T + c)
                        dve.scalar_tensor_tensor(out=junk[0:P, 0:c + 1, 0:P], in0=tiles(bank, P)[:, 0:c + 1, 0:P],
                                                 scalar=dcol[g.u][0:P, c:c + 1], in1=early[0:P, T - 1 - c:T, 0:P],
                                                 op0=ALU.is_equal, op1=ALU.mult,
                                                 accum_out=before[g.u][0:P, c:c + 1]).then_inc(s_before, 1)
                    if from_group(g, 1):
                        dve.wait_ge(s_shift, g.n)
                    dve.tensor_tensor(away[0:P, :], dumprow[0:P, :], dcol[g.u][0:P, :], ALU.subtract)\
                       .then_inc(s_away, 1)
                    dve.wait_ge(s_away, g.n + 1)
                    dve.wait_ge(s_before, (g.n + 1) * T)
                    if from_group(g, 1):
                        dve.wait_ge(s_tgt, g.n)
                    dve.scalar_tensor_tensor(out=shift[0:P, :], in0=before[g.u][0:P, :], scalar=1.0,
                                             in1=away[0:P, :], op0=ALU.min, op1=ALU.mult).then_inc(s_shift, 1)
                    dve.wait_ge(s_shift, g.n + 1)
                    if from_group(g, 2):
                        dve.wait_ge(s_scat[g.u], g.h * (16 * T))
                    dve.tensor_tensor(tgt[g.u][0:P, :], shift[0:P, :], dcol[g.u][0:P, :], ALU.add).then_inc(s_tgt, 1)
                    dve.wait_ge(s_tgt, g.n + 1)
                    dve.tensor_copy(tgts[0:P, bass.ds(g.n * T, T)], tgt[g.u][0:P, :]).then_inc(s_keep, 1)
                over_groups(dve, step)

            @block.tensor
            def _(pe):
                def spread(g):
                    pe.wait_ge(s_dcol, g.n + 1)
                    if from_group(g, 2):
                        pe.wait_ge(s_keep, g.n - 1)
                    spread_dst(pe, g, banks[:, g.u, :], s_spread)

                spread(Group(0, 0, 0, 128))

                def step(g):
                    if near(g, 1):
                        spread(near(g, 1))
                    pe.wait_ge(s_same, (g.n + 1) * T)
                    pe.wait_ge(s_feat[g.u], (g.h + 1) * 16)
                    if from_group(g, 2):
                        pe.wait_ge(s_sums, g.n - 1)
                    sum_same(pe, g, feat[g.u], WM, banks[:, 2 + 2 * g.u:4 + 2 * g.u, :], s_mm)
                over_groups(pe, step)

        class Norm:

            def __init__(self, sem, name, kind):
                self.col = 1 + kind
                self.st = sb(f"norm{kind}st", [128, T, 6])
                self.mv, self.rs, self.nm = ([sb(f"norm{kind}{n}{u}", [128, T, w]) for u in range(2)]
                                             for n, w in (("mv", 2), ("rs", 1), ("nm", 1)))
                self.sd, self.t1, self.t2 = (sb(f"norm{kind}{n}", [128, T]) for n in ("sd", "t1", "t2"))
                self.s_carry = sem(name + "_carry")
                self.s_st = sem(name + "_stats")
                self.s_mv = sem(name + "_meanvar")
                self.s_ln = sem(name + "_lnvar")
                self.s_sd = sem(name + "_root")
                self.s_t1 = sem(name + "_newton1")
                self.s_t2 = sem(name + "_newton2")
                self.s_rs = sem(name + "_rstd")
                self.s_nm = sem(name + "_bias")
                self.s_out = sem(name + "_normed")

        def norm_stats(dve, N, g, y):
            P = g.P
            if from_group(g, 1):
                dve.wait_ge(N.s_mv, g.n)
            for c in range(T):
                last = dve.bn_stats(N.st[0:P, c, :], y[:, c, :])
            last.then_inc(N.s_st, 1)
            dve.wait_ge(N.s_st, g.n + 1)
            if from_group(g, 2):
                dve.wait_ge(N.s_out, g.n - 1)
            carry_wait(dve, g, N.col, N.s_carry)
            for c in range(T):
                last = dve.bn_aggr(N.mv[g.u][0:P, c, :], N.st[0:P, c, :])
            last.then_inc(N.s_mv, 1)

        def norm_root(act, N, g):
            act.wait_ge(N.s_mv, g.n + 1)
            if from_group(g, 1):
                act.wait_ge(N.s_rs, g.n)
            act.activation(N.sd[0:g.P, :], N.mv[g.u][0:g.P, :, 1], ACT.Sqrt, bias=eps[0:g.P, :]).then_inc(N.s_sd, 1)

        def norm_recip(dve, N, g):
            dve.wait_ge(N.s_sd, g.n + 1)
            dve.reciprocal(N.rs[g.u][0:g.P, :, 0], N.sd[0:g.P, :]).then_inc(N.s_rs, 1)

        def norm_root_exp(act, N, g):
            act.wait_ge(N.s_mv, g.n + 1)
            if from_group(g, 1):
                act.wait_ge(N.s_rs, g.n)
            act.activation(N.t1[0:g.P, :], N.mv[g.u][0:g.P, :, 1], ACT.Ln, bias=eps[0:g.P, :]).then_inc(N.s_ln, 1)
            act.wait_ge(N.s_ln, g.n + 1)
            act.activation(N.sd[0:g.P, :], N.t1[0:g.P, :], ACT.Exp, scale=-0.5).then_inc(N.s_sd, 1)

        def norm_newton(dve, N, g):
            P = g.P
            dve.wait_ge(N.s_sd, g.n + 1)
            dve.scalar_tensor_tensor(out=N.t2[0:P, :], in0=N.mv[g.u][0:P, :, 1], scalar=EPS, in1=N.sd[0:P, :],
                                     op0=ALU.add, op1=ALU.mult).then_inc(N.s_t1, 1)
            dve.wait_ge(N.s_t1, g.n + 1)
            dve.scalar_tensor_tensor(out=N.t2[0:P, :], in0=N.t2[0:P, :], scalar=-0.5, in1=N.sd[0:P, :],
                                     op0=ALU.mult, op1=ALU.mult).then_inc(N.s_t2, 1)
            dve.wait_ge(N.s_t2, g.n + 1)
            dve.scalar_tensor_tensor(out=N.rs[g.u][0:P, :, 0], in0=N.t2[0:P, :], scalar=1.5, in1=N.sd[0:P, :],
                                     op0=ALU.add, op1=ALU.mult).then_inc(N.s_rs, 1)

        def norm_bias(dve, N, g):
            P = g.P
            dve.wait_ge(N.s_rs, g.n + 1)
            dve.scalar_tensor_tensor(out=N.nm[g.u][0:P, :, 0], in0=N.mv[g.u][0:P, :, 0], scalar=-1.0, in1=N.rs[g.u][0:P, :, 0],
                                     op0=ALU.mult, op1=ALU.mult).then_inc(N.s_nm, 1)

        def norm_apply(act, N, g, y, to):
            P = g.P
            act.wait_ge(N.s_nm, g.n + 1)
            for c in range(T):
                last = act.activation(to[:, c, :], y[:, c, :], ACT.Identity, bias=N.nm[g.u][0:P, c, :],
                                      scale=N.rs[g.u][0:P, c, :])
            last.then_inc(N.s_out, 1)

        def norm_apply_dve(dve, N, g, y, to):
            P = g.P
            dve.wait_ge(N.s_rs, g.n + 1)
            for c in range(T):
                last = dve.tensor_scalar(to[:, c, :], y[:, c, :], N.mv[g.u][0:P, c, 0:1], N.rs[g.u][0:P, c, :],
                                         ALU.subtract, ALU.mult)
            last.then_inc(N.s_out, 1)

        with ExitStack() as c2:
            sem, pair = semaphores(c2)
            xr = [sb(f"xr{u}", [128, T, D]) for u in range(2)]
            es = [sb(f"es{u}", [128, T, WM]) for u in range(2)]
            cnt = sb("cnt", [128, T])
            rc = sb("rc", [128, T])
            mean = [sb(f"mean{u}", [128, T, D]) for u in range(2)]
            xT = [sb(f"xT{u}", [128, 512]) for u in range(2)]
            mT = sb("mT", [128, 512])
            ab = sb("ab", [128, 512])
            ex = sb("ex", [128, 512])
            pos = sb("pos", [128, 512])
            soft = sb("soft", [128, 512])
            yT = [sb(f"yT{u}", [128, 512]) for u in range(2)]
            o = [sb(f"o{u}", [128, T, D]) for u in range(2)]
            N = Norm(sem, "n0", 1)
            s_x, s_es, s_st = pair("z_x"), pair("z_es"), pair("z_stored")
            s_cnt, s_rc, s_mean = sem("z_cnt"), sem("z_rc"), sem("z_mean")
            s_xt, s_mt, s_xT, s_mT = sem("z_xt"), sem("z_mt"), sem("z_xT"), sem("z_mT")
            s_h, s_ab, s_ex, s_lg = sem("z_h"), sem("z_abs"), sem("z_exp"), sem("z_log")
            s_pos, s_soft, s_yT, s_back = sem("z_pos"), sem("z_soft"), sem("z_yT"), sem("z_back")
            block = c2.enter_context(nc.Block())
            PX, PM, PH, PL, PB = 0, 1, 2, 3, 4

            LAG = 5

            @block.sync
            def _(sp):
                def step(g):
                    if near(g, 0):
                        if from_group(g, 2):
                            sp.wait_ge(s_mean, g.n - 1)
                        sp.dma_start(es[g.u][0:g.P, :, :],
                                     rows_of(edge_sum, g, WM).rearrange("p (c f) -> p c f", c=T))\
                          .then_inc(s_es[g.u], 16)
                        if from_group(g, 2):
                            sp.wait_ge(s_xt, g.n - 1)
                        sp.dma_start(xr[g.u][0:g.P, :, :], rows_of(a["x"], g, D).rearrange("p (c f) -> p c f", c=T))\
                          .then_inc(s_x[g.u], 16)
                over_groups(sp, step)

            @block.gpsimd
            def _(pool):
                def means(g):
                    P = g.P
                    pool.wait_ge(s_rc, g.n + 1)
                    if from_group(g, 2):
                        pool.wait_ge(s_mt, g.n - 1)
                    pool.tensor_tensor(mean[g.u][0:P, :, :], es[g.u][0:P, :, 0:D],
                                       rc[0:P, :].unsqueeze(2).to_broadcast([P, T, D]), ALU.mult).then_inc(s_mean, 1)

                def residual(g):
                    W = T * g.P
                    pool.wait_ge(s_soft, g.n + 1)
                    pool.wait_ge(s_xT, g.n + 1)
                    if from_group(g, 2):
                        pool.wait_ge(s_back, g.n - 1)
                    pool.tensor_tensor(yT[g.u][:, 0:W], soft[:, 0:W], xT[g.u][:, 0:W], ALU.add).then_inc(s_yT, 1)

                def step(g):
                    if near(g, 0):
                        means(g)
                    if near(g, -2):
                        residual(near(g, -2))
                over_groups(pool, step, LAG)

            @block.tensor
            def _(pe):
                def turn(g):
                    P = g.P
                    pe.wait_ge(s_x[g.u], (g.h + 1) * 16)
                    if from_group(g, 1):
                        pe.wait_ge(s_xT, g.n)
                    for c in range(T):
                        last = pe.transpose(banks[:, PX, c * P:(c + 1) * P], xr[g.u][0:P, c, :], ident[0:P, 0:P])
                    last.then_inc(s_xt, 1)
                    pe.wait_ge(s_mean, g.n + 1)
                    if from_group(g, 1):
                        pe.wait_ge(s_mT, g.n)
                    for c in range(T):
                        last = pe.transpose(banks[:, PM, c * P:(c + 1) * P], mean[g.u][0:P, c, :], ident[0:P, 0:P])
                    last.then_inc(s_mt, 1)

                def product(g):
                    W = T * g.P
                    pe.wait_ge(s_xT, g.n + 1)
                    if from_group(g, 1):
                        pe.wait_ge(s_pos, g.n)
                    pe.matmul(banks[:, PH, 0:W], wxT[:, :], xT[g.u][:, 0:W], start=True, stop=False)
                    pe.wait_ge(s_mT, g.n + 1)
                    pe.matmul(banks[:, PH, 0:W], weT[:, :], mT[:, 0:W], start=False, stop=True).then_inc(s_h, 1)

                def back(g):
                    P = g.P
                    pe.wait_ge(s_yT, g.n + 1)
                    if from_group(g, 2):
                        pe.wait_ge(N.s_out, g.n - 1)
                    for c in range(T):
                        last = pe.transpose(banks[0:P, PB + g.u, c * 128:(c + 1) * 128], yT[g.u][:, c * P:(c + 1) * P],
                                            ident[:, :])
                    last.then_inc(s_back, 1)

                def step(g):
                    if near(g, -1):
                        turn(near(g, -1))
                    if near(g, -3):
                        back(near(g, -3))
                    if near(g, -1):
                        product(near(g, -1))
                over_groups(pe, step, LAG)

            @block.scalar
            def _(act):
                def turn(g):
                    W = T * g.P
                    act.wait_ge(s_xt, g.n + 1)
                    if from_group(g, 2):
                        act.wait_ge(s_yT, g.n - 1)
                    act.activation(xT[g.u][:, 0:W], banks[:, PX, 0:W], ACT.Copy).then_inc(s_xT, 1)

                def absolute(g):
                    W = T * g.P
                    act.wait_ge(s_h, g.n + 1)
                    if from_group(g, 1):
                        act.wait_ge(s_ex, g.n)
                    act.activation(ab[:, 0:W], banks[:, PH, 0:W], ACT.Abs, bias=gvec[:, :]).then_inc(s_ab, 1)

                def softplus(g):
                    W = T * g.P
                    act.wait_ge(s_ab, g.n + 1)
                    if from_group(g, 1):
                        act.wait_ge(s_lg, g.n)
                    act.activation(ex[:, 0:W], ab[:, 0:W], ACT.Exp, scale=-1.0).then_inc(s_ex, 1)
                    act.wait_ge(s_ex, g.n + 1)
                    if from_group(g, 1):
                        act.wait_ge(s_soft, g.n)
                    act.activation(banks[:, PL, 0:W], ex[:, 0:W], ACT.Ln, bias=ones[:, 0:1]).then_inc(s_lg, 1)

                def store(g):
                    act.wait_ge(N.s_out, g.n + 1)
                    act.dma_start(rows_of(x1, g, D), o[g.u][0:g.P, :, :].rearrange("p c f -> p (c f)"))\
                       .then_inc(s_st[g.u], 16)

                def norm(g):
                    if from_group(g, 2):
                        act.wait_ge(s_st[g.u], g.h * 16)
                    norm_apply(act, N, g, tiles(banks[:, PB + g.u, :], g.P), o[g.u][0:g.P, :, :])

                def root(g):
                    norm_root_exp(act, N, g)

                def step(g):
                    for d, part in ((-2, absolute), (-4, norm), (-1, turn), (-2, softplus), (-5, store), (-3, root)):
                        if near(g, d):
                            part(near(g, d))
                act.preload_act_table_set("natural_log_exp_and_others")
                over_groups(act, step, LAG)
                for u in range(2):
                    act.wait_ge(s_st[u], GROUPS // 2 * 16)

            @block.vector
            def _(dve):
                def counts(g):
                    P = g.P
                    dve.wait_ge(s_es[g.u], (g.h + 1) * 16)
                    if from_group(g, 1):
                        dve.wait_ge(s_rc, g.n)
                    dve.tensor_scalar(cnt[0:P, :], es[g.u][0:P, :, D], 1.0, None, ALU.max).then_inc(s_cnt, 1)
                    dve.wait_ge(s_cnt, g.n + 1)
                    if from_group(g, 1):
                        dve.wait_ge(s_mean, g.n)
                    dve.reciprocal(rc[0:P, :], cnt[0:P, :]).then_inc(s_rc, 1)

                def turn(g):
                    W = T * g.P
                    dve.wait_ge(s_mt, g.n + 1)
                    if from_group(g, 1):
                        dve.wait_ge(s_h, g.n)
                    dve.tensor_copy(mT[:, 0:W], banks[:, PM, 0:W]).then_inc(s_mT, 1)

                def positive(g):
                    W = T * g.P
                    dve.wait_ge(s_ab, g.n + 1)
                    if from_group(g, 1):
                        dve.wait_ge(s_soft, g.n)
                    dve.tensor_scalar(pos[:, 0:W], banks[:, PH, 0:W], gvec[:, 0:1], 0.0, ALU.add, ALU.max)\
                       .then_inc(s_pos, 1)

                def softplus(g):
                    W = T * g.P
                    dve.wait_ge(s_pos, g.n + 1)
                    dve.wait_ge(s_lg, g.n + 1)
                    if from_group(g, 1):
                        dve.wait_ge(s_yT, g.n)
                    dve.scalar_tensor_tensor(out=soft[:, 0:W], in0=pos[:, 0:W], scalar=-math.log(2.0),
                                             in1=banks[:, PL, 0:W], op0=ALU.add, op1=ALU.add).then_inc(s_soft, 1)

                def stats(g):
                    dve.wait_ge(s_back, g.n + 1)
                    norm_stats(dve, N, g, tiles(banks[:, PB + g.u, :], g.P))

                def rstd(g):
                    norm_newton(dve, N, g)
                    norm_bias(dve, N, g)

                def step(g):
                    for d, part in ((-4, rstd), (0, counts), (-2, positive), (-1, turn), (-3, stats), (-2, softplus)):
                        if near(g, d):
                            part(near(g, d))
                over_groups(dve, step, LAG)

        def edges(l, table):
            with ExitStack() as c2:
                sem, pair = semaphores(c2, f"a{l}_")

                isrc = [sb(f"isrc{u}", [128, T], I32) for u in range(2)]
                idst = [sb(f"idst{u}", [128, T], I32) for u in range(2)]
                hs = [sb(f"hs{u}", [128, T, D]) for u in range(2)]
                hd = [sb(f"hd{u}", [128, T, D]) for u in range(2)]
                hsT, hdT, kT, prod = (sb(n, [128, 512]) for n in ("hsT", "hdT", "kT", "prod"))
                clip = sb("clip", [128, T * HEADS])
                vals = sb("vals", [128, T, WA])
                sums = [sb(f"asums{u}", [128, T * WA]) for u in range(2)]
                s_ix, s_it, s_dcol, s_spread, s_same = sem("ix"), sem("it"), sem("dcol"), sem("spread"), sem("same")
                s_gat, s_scat = a_gathered[l], a_scattered[l]
                s_st, s_dt, s_hsT, s_hdT = sem("st"), sem("dt"), sem("hsT"), sem("hdT")
                s_k, s_q, s_v, s_kT, s_prod = sem("k"), sem("q"), sem("v"), sem("kT"), sem("prod")
                s_sc, s_clip, s_w, s_vals = sem("score"), sem("clip"), sem("weight"), sem("vals")
                s_mm, s_sums = sem("summed"), sem("sums")
                s_carry_g, s_carry_s = sem("carry_gather"), sem("carry_scatter")
                block = c2.enter_context(nc.Block())
                PS, PT, PK, PQ, PV, PD = 0, 1, 2, 3, 4, 5
                A = banks[:, 6:8, :]
                SC = banks[:, 7, 512 - T * HEADS:512]

                @block.gpsimd
                def _(pool):
                    def gather(g, c):
                        P = g.P
                        if c == 0:
                            pool.wait_ge(s_ix, 2 * (g.n + 1))
                            if from_group(g, 2):
                                pool.wait_ge(s_dt, g.n - 1)
                            carry_wait(pool, g, 0, s_carry_g)
                        for ix, to in ((isrc, hs), (idst, hd)):
                            pool.indirect_dma_start(to[g.u][0:P, c, :], None, table,
                                                    bass.IndirectOffsetOnAxis(ix[g.u][0:P, c:c + 1], 0))\
                                .then_inc(s_gat[g.u], 16)

                    def scatter(g, c):
                        if c == 0:
                            pool.wait_ge(s_it, g.n + 1)
                            pool.wait_ge(s_sums, g.n + 1)
                            if from_group(g, 1):
                                p = near(g, -1)
                                pool.wait_ge(s_scat[p.u], (p.h + 1) * (16 * T))
                            carry_wait(pool, g, 1, s_carry_s)
                        pool.indirect_dma_start(attn_sum[l], bass.IndirectOffsetOnAxis(tgt[g.u][0:g.P, c:c + 1], 0),
                                                sums[g.u][0:g.P, c * WA:(c + 1) * WA], None, compute_op=ALU.add)\
                            .then_inc(s_scat[g.u], 16)

                    for c in range(T):
                        gather(Group(0, 0, 0, 128), c)

                    def step(g):
                        for c in range(T):
                            if near(g, 1):
                                gather(near(g, 1), c)
                        for c in range(T):
                            if near(g, -1):
                                scatter(near(g, -1), c)
                    over_groups(pool, step)
                    for c in range(T):
                        scatter(near(Group(GROUPS, 0, 0, 0), -1), c)
                    for u in range(2):
                        pool.wait_ge(s_scat[u], GROUPS // 2 * 16 * T)

                @block.vector
                def _(dve):
                    def indices(g):
                        dve.tensor_copy(isrc[g.u][0:g.P, :], srcs[0:g.P, bass.ds(g.n * T, T)]).then_inc(s_ix, 1)
                        dve.tensor_copy(idst[g.u][0:g.P, :], dsts[0:g.P, bass.ds(g.n * T, T)]).then_inc(s_ix, 1)

                    indices(Group(0, 0, 0, 128))
                    indices(Group(1, 0, 1, 128))

                    def matrix(g):
                        dve.wait_ge(s_spread, g.n + 1)
                        dve.wait_ge(s_dcol, g.n + 1)
                        if from_group(g, 2):
                            dve.wait_ge(s_mm, g.n - 1)
                        build_same(dve, g, banks[:, PD, :], s_same)
                        if near(g, 1):
                            if from_group(g, 1):
                                dve.wait_ge(s_same, T * g.n)
                                dve.wait_ge(s_spread, g.n)
                            copy_dst(dve, near(g, 1), s_dcol)

                    copy_dst(dve, Group(0, 0, 0, 128), s_dcol)
                    matrix(Group(0, 0, 0, 128))

                    def step(g):
                        P, W = g.P, T * g.P
                        if from_group(g, 2):
                            dve.wait_ge(s_scat[g.u], g.h * (16 * T))
                        dve.tensor_copy(tgt[g.u][0:P, :], tgts[0:P, bass.ds(g.n * T, T)]).then_inc(s_it, 1)
                        dve.wait_ge(s_gat[g.u], (g.h + 1) * (32 * T))
                        if near(g, 2):
                            indices(near(g, 2))
                        dve.wait_ge(s_dt, g.n + 1)
                        if from_group(g, 1):
                            dve.wait_ge(s_q, g.n)
                        dve.tensor_copy(hdT[:, 0:W], banks[:, PT, 0:W]).then_inc(s_hdT, 1)
                        if near(g, 1):
                            matrix(near(g, 1))
                        dve.wait_ge(s_q, g.n + 1)
                        dve.wait_ge(s_kT, g.n + 1)
                        if from_group(g, 1):
                            dve.wait_ge(s_sc, g.n)
                        dve.scalar_tensor_tensor(out=prod[:, 0:W], in0=banks[:, PQ, 0:W], scalar=bq[:, l:l + 1],
                                                 in1=kT[:, 0:W], op0=ALU.add, op1=ALU.mult).then_inc(s_prod, 1)
                        dve.wait_ge(s_sc, g.n + 1)
                        if from_group(g, 1):
                            dve.wait_ge(s_w, g.n)
                        dve.tensor_scalar(clip[0:P, :], SC[0:P, :], -5.0, 5.0, ALU.max, ALU.min).then_inc(s_clip, 1)
                        dve.wait_ge(s_w, g.n + 1)
                        dve.wait_ge(s_v, g.n + 1)
                        weight = vals[0:P, :, D:WA].unsqueeze(3).to_broadcast([P, T, HEADS, DK])
                        dve.tensor_tensor(vals[0:P, :, 0:D].rearrange("p c (h k) -> p c h k", h=HEADS),
                                          banks[0:P, PV, :].rearrange("p (c h k) -> p c h k", c=T, h=HEADS),
                                          weight, ALU.mult).then_inc(s_vals, 1)
                    over_groups(dve, step)

                @block.scalar
                def _(act):
                    def weigh(g):
                        P, W = g.P, T * g.P
                        act.wait_ge(s_st, g.n + 1)
                        if from_group(g, 1):
                            act.wait_ge(s_v, g.n)
                        act.activation(hsT[:, 0:W], banks[:, PS, 0:W], ACT.Copy).then_inc(s_hsT, 1)
                        act.wait_ge(s_k, g.n + 1)
                        if from_group(g, 1):
                            act.wait_ge(s_prod, g.n)
                        act.activation(kT[:, 0:W], banks[:, PK, 0:W], ACT.Identity, bias=bk[:, l:l + 1])\
                           .then_inc(s_kT, 1)

                    def exponential(g):
                        P = g.P
                        act.wait_ge(s_clip, g.n + 1)
                        if from_group(g, 1):
                            act.wait_ge(s_mm, g.n)
                        act.activation(vals[0:P, :, D:WA], clip[0:P, :].rearrange("p (c h) -> p c h", c=T), ACT.Exp)\
                           .then_inc(s_w, 1)

                    def keep_sums(g):
                        P = g.P
                        act.wait_ge(s_mm, g.n + 1)
                        if from_group(g, 2):
                            act.wait_ge(s_scat[g.u], g.h * (16 * T))
                        act.activation(sums[g.u][0:P, :].rearrange("p (k f) -> p k f", k=2), A[0:P, :, 0:2 * WA],
                                       ACT.Copy).then_inc(s_sums, 1)

                    def step(g):
                        for d, part in ((0, weigh), (-1, keep_sums), (0, exponential)):
                            if near(g, d):
                                part(near(g, d))
                    over_groups(act, step, 1)

                @block.tensor
                def _(pe):
                    def spread(g):
                        pe.wait_ge(s_dcol, g.n + 1)
                        if from_group(g, 1):
                            pe.wait_ge(s_same, T * g.n)
                        spread_dst(pe, g, banks[:, PD, :], s_spread)

                    def turn(g):
                        P = g.P
                        pe.wait_ge(s_gat[g.u], (g.h + 1) * (32 * T))
                        if from_group(g, 1):
                            pe.wait_ge(s_hsT, g.n)
                            pe.wait_ge(s_hdT, g.n)
                        for bank, h, done in ((PS, hs, s_st), (PT, hd, s_dt)):
                            for c in range(T):
                                last = pe.transpose(banks[:, bank, c * P:(c + 1) * P], h[g.u][0:P, c, :],
                                                    ident[0:P, 0:P])
                            last.then_inc(done, 1)

                    def products(g):
                        P, W = g.P, T * g.P
                        pe.wait_ge(s_hsT, g.n + 1)
                        if from_group(g, 1):
                            pe.wait_ge(s_kT, g.n)
                        pe.matmul(banks[:, PK, 0:W], wk[:, l, :], hsT[:, 0:W], start=True, stop=True).then_inc(s_k, 1)
                        pe.wait_ge(s_hdT, g.n + 1)
                        if from_group(g, 1):
                            pe.wait_ge(s_prod, g.n)
                        pe.matmul(banks[:, PQ, 0:W], wq[:, l, :], hdT[:, 0:W], start=True, stop=True).then_inc(s_q, 1)
                        if from_group(g, 1):
                            pe.wait_ge(s_vals, g.n)
                        for c in range(T):
                            to = banks[0:P, PV, c * 128:(c + 1) * 128]
                            pe.matmul(to, hsT[:, c * P:(c + 1) * P], wv[:, l, :], start=True, stop=False)
                            last = pe.matmul(to, ones[0:1, 0:P], bv[:, l, :], start=False, stop=True)
                        last.then_inc(s_v, 1)

                    def scores(g):
                        P = g.P
                        pe.wait_ge(s_prod, g.n + 1)
                        if from_group(g, 1):
                            pe.wait_ge(s_clip, g.n)
                            pe.wait_ge(s_sums, g.n)
                        for c in range(T):
                            last = pe.matmul(SC[0:P, c * HEADS:(c + 1) * HEADS], prod[:, c * P:(c + 1) * P],
                                             heads[:, :], start=True, stop=True)
                        last.then_inc(s_sc, 1)

                    def sums_of(g):
                        pe.wait_ge(s_vals, g.n + 1)
                        pe.wait_ge(s_same, T * (g.n + 1))
                        pe.wait_ge(s_clip, g.n + 1)
                        if from_group(g, 1):
                            pe.wait_ge(s_sums, g.n)
                        sum_same(pe, g, vals, WA, A, s_mm)

                    spread(Group(0, 0, 0, 128))

                    def step(g):
                        for d, part in ((1, spread), (0, turn), (-1, sums_of), (0, products), (0, scores)):
                            if near(g, d):
                                part(near(g, d))
                    over_groups(pe, step, 1)

        def nodes(l, table, to_dram, last_layer):
            with ExitStack() as c2:
                sem, pair = semaphores(c2, f"n{l}_")

                ag = [sb(f"ag{u}", [128, T, WA]) for u in range(2)]
                hr = [sb(f"hr{u}", [128, T, D]) for u in range(2)]
                xs = [sb(f"xs{u}", [128, T, D]) for u in range(2)]
                z, rz = sb("z", [128, T, HEADS]), sb("rz", [128, T, HEADS])
                at = [sb(f"at{u}", [128, T, D]) for u in range(2)]
                hb = [sb(f"hb{u}", [128, T, D]) for u in range(2)]
                atT = sb("atT", [128, 512])
                y, xh = (sb(n, [128, T, D]) for n in ("y", "xh"))
                h1T, r0, r1, y2T = (sb(n, [128, 512]) for n in ("h1T", "r0", "r1", "y2T"))
                xo, sg, xb = (sb(n, [128, T, D]) for n in ("xo", "sg", "xb"))
                res = [sb(f"res{u}", [128, T, D]) for u in range(2)]
                o = [sb(f"o{u}", [128, T, D]) for u in range(2)]
                N1, N2 = Norm(sem, f"n{l}a", 1), Norm(sem, f"n{l}b", 2)
                N3 = Norm(sem, f"n{l}c", 3) if last_layer else None
                s_ag, s_hr, s_xs, s_st = pair("ag"), pair("hr"), pair("xs"), pair("stored")
                s_z, s_rz, s_at, s_hb = sem("z"), sem("rz"), sem("at"), sem("hb")
                s_att, s_atT, s_wo, s_y = sem("att"), sem("atT"), sem("wo"), sem("y")
                s_xt, s_h1T, s_w1, s_r0, s_r1 = sem("xt"), sem("h1T"), sem("w1"), sem("r0"), sem("r1")
                s_w2, s_y2T, s_back, s_sg, s_o, s_xb = (sem(n) for n in ("w2", "y2T", "back", "sg", "o", "xb"))
                block = c2.enter_context(nc.Block())
                PA, PW, PX, PR0, PR1, PF, PB = range(7)
                out_ready = N3.s_out if last_layer else s_o

                LAG = 7

                @block.sync
                def _(sp):
                    def step(g):
                        if near(g, 0):
                            if from_group(g, 2):
                                sp.wait_ge(s_at, g.n - 1)
                            sp.dma_start(ag[g.u][0:g.P, :, :],
                                         rows_of(attn_sum[l], g, WA).rearrange("p (c f) -> p c f", c=T))\
                              .then_inc(s_ag[g.u], 16)
                            if from_group(g, 2):
                                sp.wait_ge(s_hb, g.n - 1)
                            sp.dma_start(hr[g.u][0:g.P, :, :], rows_of(table, g, D).rearrange("p (c f) -> p c f", c=T))\
                              .then_inc(s_hr[g.u], 16)
                        p = near(g, -4)
                        if last_layer and p:
                            if from_group(p, 2):
                                sp.wait_ge(s_xb, p.n - 1)
                            sp.dma_start(xs[p.u][0:p.P, :, :], rows_of(x1, p, D).rearrange("p (c f) -> p c f", c=T))\
                              .then_inc(s_xs[p.u], 16)
                    over_groups(sp, step, LAG)

                @block.gpsimd
                def _(pool):
                    def divide(g):
                        P = g.P
                        pool.wait_ge(s_rz, g.n + 1)
                        if from_group(g, 2):
                            pool.wait_ge(s_att, g.n - 1)
                        pool.tensor_tensor(at[g.u][0:P, :, :].rearrange("p c (h k) -> p c h k", h=HEADS),
                                           ag[g.u][0:P, :, 0:D].rearrange("p c (h k) -> p c h k", h=HEADS),
                                           rz[0:P, :, :].unsqueeze(3).to_broadcast([P, T, HEADS, DK]), ALU.mult)\
                            .then_inc(s_at, 1)
                        pool.wait_ge(s_hr[g.u], (g.h + 1) * 16)
                        if from_group(g, 2):
                            pool.wait_ge(s_y, g.n - 1)
                        pool.tensor_tensor(hb[g.u][0:P, :, :], hr[g.u][0:P, :, :],
                                           bo[0:P, l, :].unsqueeze(1).to_broadcast([P, T, D]), ALU.add)\
                            .then_inc(s_hb, 1)

                    def gain(g):
                        P = g.P
                        if last_layer:
                            pool.wait_ge(s_xs[g.u], (g.h + 1) * 16)
                            if from_group(g, 1):
                                pool.wait_ge(s_o, g.n)
                            pool.tensor_tensor(xb[0:P, :, :], xs[g.u][0:P, :, :],
                                               be2[0:P, l, :].unsqueeze(1).to_broadcast([P, T, D]), ALU.add)\
                                .then_inc(s_xb, 1)
                        pool.wait_ge(N2.s_out, g.n + 1)
                        if from_group(g, 1):
                            pool.wait_ge(s_o, g.n)
                        pool.tensor_tensor(sg[0:P, :, :], xo[0:P, :, :],
                                           g2[0:P, l, :].unsqueeze(1).to_broadcast([P, T, D]), ALU.mult)\
                            .then_inc(s_sg, 1)
                        pool.wait_ge(s_sg, g.n + 1)
                        if last_layer:
                            pool.wait_ge(s_xb, g.n + 1)
                            to, add = res[g.u], xb[0:P, :, :]
                        else:
                            to, add = o[g.u], be2[0:P, l, :].unsqueeze(1).to_broadcast([P, T, D])
                        if from_group(g, 2):
                            if last_layer:
                                pool.wait_ge(N3.s_out, g.n - 1)
                            else:
                                pool.wait_ge(s_st[g.u], g.h * 16)
                        pool.tensor_tensor(to[0:P, :, :], sg[0:P, :, :], add, ALU.add).then_inc(s_o, 1)

                    def step(g):
                        if near(g, 0):
                            divide(g)
                        if near(g, -4):
                            gain(near(g, -4))
                    over_groups(pool, step, LAG)

                @block.tensor
                def _(pe):
                    def attn(g):
                        P = g.P
                        pe.wait_ge(s_at, g.n + 1)
                        if from_group(g, 1):
                            pe.wait_ge(s_atT, g.n)
                        for c in range(T):
                            last = pe.transpose(banks[:, PA, c * P:(c + 1) * P], at[g.u][0:P, c, :], ident[0:P, 0:P])
                        last.then_inc(s_att, 1)

                    def project(g):
                        P = g.P
                        pe.wait_ge(s_atT, g.n + 1)
                        if from_group(g, 1):
                            pe.wait_ge(s_y, g.n)
                        for c in range(T):
                            last = pe.matmul(banks[0:P, PW, c * 128:(c + 1) * 128], atT[:, c * P:(c + 1) * P],
                                             wo[:, l, :], start=True, stop=True)
                        last.then_inc(s_wo, 1)

                    def turn(g):
                        P = g.P
                        pe.wait_ge(N1.s_out, g.n + 1)
                        if from_group(g, 1):
                            pe.wait_ge(s_h1T, g.n)
                        for c in range(T):
                            last = pe.transpose(banks[:, PX, c * P:(c + 1) * P], xh[0:P, c, :], ident[0:P, 0:P])
                        last.then_inc(s_xt, 1)

                    def up(g):
                        W = T * g.P
                        pe.wait_ge(s_h1T, g.n + 1)
                        for k, (bank, used) in enumerate(((PR0, s_r0), (PR1, s_r1))):
                            if from_group(g, 1):
                                pe.wait_ge(used, g.n)
                            pe.matmul(banks[:, bank, 0:W], w1[:, l, 128 * k:128 * (k + 1)], h1T[:, 0:W],
                                      start=True, stop=True).then_inc(s_w1, 1)

                    def down(g):
                        W = T * g.P
                        pe.wait_ge(s_r0, g.n + 1)
                        if from_group(g, 1):
                            pe.wait_ge(s_y2T, g.n)
                        pe.matmul(banks[:, PF, 0:W], w2[:, l, 0, :], r0[:, 0:W], start=True, stop=False)
                        pe.wait_ge(s_r1, g.n + 1)
                        pe.matmul(banks[:, PF, 0:W], w2[:, l, 1, :], r1[:, 0:W], start=False, stop=True)\
                          .then_inc(s_w2, 1)

                    def back(g):
                        P = g.P
                        pe.wait_ge(s_y2T, g.n + 1)
                        if from_group(g, 2):
                            pe.wait_ge(N2.s_out, g.n - 1)
                        for c in range(T):
                            last = pe.transpose(banks[0:P, PB + g.u, c * 128:(c + 1) * 128], y2T[:, c * P:(c + 1) * P],
                                                ident[:, :])
                        last.then_inc(s_back, 1)

                    def step(g):
                        for d, part in ((-1, attn), (-2, turn), (-1, project), (-3, back), (-2, up), (-2, down)):
                            if near(g, d):
                                part(near(g, d))
                    over_groups(pe, step, LAG)

                @block.scalar
                def _(act):
                    def attn(g):
                        W = T * g.P
                        act.wait_ge(s_att, g.n + 1)
                        if from_group(g, 1):
                            act.wait_ge(s_wo, g.n)
                        act.activation(atT[:, 0:W], banks[:, PA, 0:W], ACT.Copy).then_inc(s_atT, 1)

                    def scale(g):
                        W = T * g.P
                        act.wait_ge(s_xt, g.n + 1)
                        if from_group(g, 1):
                            act.wait_ge(s_y2T, g.n)
                        act.activation(h1T[:, 0:W], banks[:, PX, 0:W], ACT.Identity, bias=be1[:, l:l + 1],
                                       scale=g1[:, l:l + 1]).then_inc(s_h1T, 1)

                    def relu(g):
                        W = T * g.P
                        for k, (r, bank, done) in enumerate(((r0, PR0, s_r0), (r1, PR1, s_r1))):
                            act.wait_ge(s_w1, 2 * g.n + 1 + k)
                            if from_group(g, 1):
                                act.wait_ge(s_w2, g.n)
                            act.activation(r[:, 0:W], banks[:, bank, 0:W], ACT.Relu,
                                           bias=b1[:, 2 * l + k:2 * l + k + 1]).then_inc(done, 1)

                    def root1(g):
                        norm_root(act, N1, g)

                    def root2(g):
                        norm_root(act, N2, g)

                    def root3(g):
                        norm_root(act, N3, g)

                    def store(g):
                        act.wait_ge(out_ready, g.n + 1)
                        act.dma_start(rows_of(to_dram, g, D), o[g.u][0:g.P, :, :].rearrange("p c f -> p (c f)"))\
                           .then_inc(s_st[g.u], 16)

                    def norm2(g):
                        if from_group(g, 1):
                            act.wait_ge(s_sg, g.n)
                        norm_apply(act, N2, g, tiles(banks[:, PB + g.u, :], g.P), xo[0:g.P, :, :])

                    def norm3(g):
                        if from_group(g, 2):
                            act.wait_ge(s_st[g.u], g.h * 16)
                        norm_apply(act, N3, g, res[g.u][0:g.P, :, :], o[g.u][0:g.P, :, :])

                    if last_layer:
                        order = [(-1, attn), (-4, norm2), (-2, scale), (-6, norm3), (-2, relu), (-7, store),
                                 (-1, root1), (-5, root3), (-3, root2)]
                    else:
                        order = [(-5, store), (-1, attn), (-4, norm2), (-2, scale), (-1, root1), (-2, relu),
                                 (-3, root2)]

                    def step(g):
                        for d, part in order:
                            if near(g, d):
                                part(near(g, d))
                    over_groups(act, step, LAG)
                    for u in range(2):
                        act.wait_ge(s_st[u], GROUPS // 2 * 16)

                @block.vector
                def _(dve):
                    def recip_z(g):
                        P = g.P
                        dve.wait_ge(s_ag[g.u], (g.h + 1) * 16)
                        if from_group(g, 1):
                            dve.wait_ge(s_rz, g.n)
                        dve.tensor_scalar(z[0:P, :, :], ag[g.u][0:P, :, D:WA], 1e-6, None, ALU.add).then_inc(s_z, 1)
                        dve.wait_ge(s_z, g.n + 1)
                        if from_group(g, 1):
                            dve.wait_ge(s_at, g.n)
                        dve.reciprocal(rz[0:P, :, :], z[0:P, :, :]).then_inc(s_rz, 1)

                    def stats1(g):
                        P = g.P
                        dve.wait_ge(s_wo, g.n + 1)
                        dve.wait_ge(s_hb, g.n + 1)
                        if from_group(g, 1):
                            dve.wait_ge(N1.s_out, g.n)
                        dve.tensor_tensor(y[0:P, :, :], tiles(banks[:, PW, :], P), hb[g.u][0:P, :, :], ALU.add)\
                           .then_inc(s_y, 1)
                        dve.wait_ge(s_y, g.n + 1)
                        norm_stats(dve, N1, g, y[0:P, :, :])

                    def norm1(g):
                        norm_recip(dve, N1, g)
                        if from_group(g, 1):
                            dve.wait_ge(s_xt, g.n)
                        norm_apply_dve(dve, N1, g, y[0:g.P, :, :], xh[0:g.P, :, :])

                    def residual(g):
                        W = T * g.P
                        dve.wait_ge(s_w2, g.n + 1)
                        dve.wait_ge(s_h1T, g.n + 1)
                        if from_group(g, 1):
                            dve.wait_ge(s_back, g.n)
                        dve.scalar_tensor_tensor(out=y2T[:, 0:W], in0=banks[:, PF, 0:W], scalar=b2[:, l:l + 1],
                                                 in1=h1T[:, 0:W], op0=ALU.add, op1=ALU.add).then_inc(s_y2T, 1)

                    def stats2(g):
                        dve.wait_ge(s_back, g.n + 1)
                        norm_stats(dve, N2, g, tiles(banks[:, PB + g.u, :], g.P))

                    def rstd2(g):
                        norm_recip(dve, N2, g)
                        norm_bias(dve, N2, g)

                    def stats3(g):
                        dve.wait_ge(s_o, g.n + 1)
                        norm_stats(dve, N3, g, res[g.u][0:g.P, :, :])

                    def rstd3(g):
                        norm_recip(dve, N3, g)
                        norm_bias(dve, N3, g)

                    order = [(-2, norm1), (-4, rstd2), (0, recip_z), (-3, residual), (-1, stats1), (-3, stats2)]
                    if last_layer:
                        order = [(-2, norm1), (-4, rstd2), (-3, residual), (0, recip_z), (-6, rstd3), (-5, stats3),
                                 (-1, stats1), (-3, stats2)]

                    def step(g):
                        for d, part in order:
                            if near(g, d):
                                part(near(g, d))
                    over_groups(dve, step, LAG)

        edges(0, x1)
        nodes(0, x1, h1, False)
        edges(1, h1)
        nodes(1, h1, out, True)


_INS = {"x": "x", "src": "src", "dst": "dst", "edge_attr_128": "edge", "L0_gnn_global_feats": "glob", "L0_gnn_W": "W"}
_INS.update({f"L1_gnn_{n}": n for n in ("Wq", "bq", "Wk", "bk", "Wv", "bv", "Wo", "bo", "W1", "b1", "W2", "b2",
                                        "ln1_g", "ln1_b", "ln2_g", "ln2_b")})


def kernel(**inputs):
    import numpy as _np
    import concourse.bacc as _bacc
    from concourse import mybir as _mybir
    from concourse.bass_utils import run_bass_kernel_spmd as _run

    nc = _bacc.Bacc("TRN2", target_bir_lowering=False, num_devices=1)
    arrays, args = {}, {}
    for name, short in _INS.items():
        v = _np.ascontiguousarray(inputs[name])
        arrays[f"in_{name}"] = v
        args[short] = nc.dram_tensor(f"in_{name}", v.shape, _mybir.dt.from_np(v.dtype), kind="ExternalInput").ap()
    out = nc.dram_tensor("out_0", (NODES, D), F32, kind="ExternalOutput").ap()
    program(nc, args, out)
    r = _run(nc, [arrays], core_ids=[0])
    return r.results[0]["out_0"]
```

```python
from collections import namedtuple
from contextlib import ExitStack
import math

import concourse.bass as bass
from concourse import mybir

F32 = mybir.dt.float32
I32 = mybir.dt.int32
ALU = mybir.AluOpType
ACT = mybir.ActivationFunctionType

NODES = 50000
D = 128
HEADS = 8
DK = D // HEADS
LAYERS = 2
T = 4
ROWS = 128 * T
FULL = NODES // ROWS
TAIL = (NODES - FULL * ROWS) // T
GROUPS = FULL + 1
CHUNKS = GROUPS + 1
PAD = CHUNKS * ROWS
DUMP = GROUPS * ROWS
NEAR = 3
WM = D + 1
WA = D + HEADS
EPS = 1e-5

assert NODES == FULL * ROWS + TAIL * T and GROUPS % 2 == 0

Group = namedtuple("Group", "n h u P")


def near(g, d):
    k = g.u + d
    n = g.n + d
    if isinstance(n, int):
        if n < 0 or n >= GROUPS:
            return None
        return Group(n, n // 2, n % 2, TAIL if n == FULL else 128)
    return Group(n, g.h + k // 2, k % 2, 128)


def from_group(g, k):
    return not isinstance(g.n, int) or g.n >= k


FIRST, LAST = 10, (GROUPS - 4) // 2 * 2


def over_groups(eng, step, lag=0, first=FIRST):
    def peeled(n):
        step(Group(n, n // 2, n % 2, TAIL if n == FULL else 128))

    for n in range(first):
        peeled(n)
    with eng.Fori(first // 2, LAST // 2) as h:
        for u in range(2):
            step(Group(h * 2 + u, h, u, 128))
    for n in range(LAST, GROUPS + lag):
        peeled(n)


def rows_of(dram, g, width):
    if isinstance(g.n, int) and g.n == FULL:
        part = dram[FULL * ROWS:NODES, :]
        return part.rearrange("(p c) f -> p (c f)", c=T)
    full = dram[0:FULL * ROWS, :].rearrange("(g p c) f -> g p (c f)", p=128, c=T)
    return full[g.n, :, :]


def clear(eng, array, zeros, landed):
    chunks = array.rearrange("(g p c) f -> g p (c f)", p=128, c=T)
    k, turns = len(landed), CHUNKS // len(landed)
    assert k * turns == CHUNKS
    for j in range(k):
        eng.dma_start(chunks[j, :, :], zeros).then_inc(landed[j], 16)
    with eng.Fori(1, turns) as h:
        for j in range(k):
            eng.wait_ge(landed[j], h * 16)
            eng.dma_start(chunks[h * k + j, :, :], zeros).then_inc(landed[j], 16)


def wait_clear(eng, landed):
    for s in landed:
        eng.wait_ge(s, 16 * (CHUNKS // len(landed)))


def tiles(t, P):
    return t[0:P, :].rearrange("p (c f) -> p c f", c=T)


def program(nc, a, out):
    with ExitStack() as ctx:
        buffers = {}

        def sb(name, shape, dt=F32):
            if name not in buffers:
                buffers[name] = ctx.enter_context(nc.sbuf_tensor(name, shape, dt))
            return buffers[name]

        def gpsimd_pair(name):
            return [ctx.enter_context(nc.semaphore(f"{name}{u}")) for u in range(2)]

        e_scattered = gpsimd_pair("e_scattered")
        a_gathered = [gpsimd_pair(f"a{l}_gathered") for l in range(LAYERS)]
        a_scattered = [gpsimd_pair(f"a{l}_scattered") for l in range(LAYERS)]
        nc.all_engine_barrier()
        first_num = nc.alloc_semaphore(name="first")
        nc.release_semaphore(first_num)

        def semaphores(phase, prefix=""):
            made = []

            def sem(name):
                made.append(phase.enter_context(nc.semaphore(prefix + name, num=first_num.num + len(made))))
                return made[-1]

            def pair(name):
                return [sem(f"{name}0"), sem(f"{name}1")]

            phase.callback(lambda: nc.all_engine_barrier(sems_to_clear=range(made[0].num, made[-1].num + 1)))
            return sem, pair

        def dram(name, rows, width):
            return nc.dram_tensor(name, (rows, width), F32, kind="Internal").ap()

        edge_sum = [dram(f"edge_sum{u}", PAD, WM) for u in range(2)]
        attn_sum = [dram(f"attn_sum{l}", PAD, WA) for l in range(LAYERS)]
        x1 = dram("x1", NODES, D)
        h1 = dram("h1", NODES, D)

        banks = ctx.enter_context(nc.psum_tensor("banks", [128, 8, 512], F32))

        ident = sb("ident", [128, 128])
        early = sb("early", [128, NEAR, 128])
        zeros = sb("zeros", [128, T * WA])
        ones = sb("ones", [128, 128])
        heads = sb("heads", [128, HEADS])
        dumprow = sb("dumprow", [128, T])
        eps = sb("eps", [128, 1])
        w0 = sb("w0", [128, 320])
        wxT = sb("wxT", [128, 128])
        weT = sb("weT", [128, 128])
        wgT = sb("wgT", [64, 128])
        glob = sb("glob", [64, 1])
        gvec = sb("gvec", [128, 1])
        wq, wk, wv, wo = (sb(f"w{n}", [128, LAYERS, 128]) for n in "qkvo")
        w1 = sb("w1", [128, LAYERS, 256])
        w2 = sb("w2", [128, LAYERS, 2, 128])
        bq, bk, b2, g1, be1 = (sb(n, [128, LAYERS]) for n in ("bq", "bk", "b2", "g1", "be1"))
        b1 = sb("b1", [128, LAYERS * 2])
        bv = sb("bv", [1, LAYERS, 128])
        bo, g2, be2 = (sb(n, [128, LAYERS, 128]) for n in ("bo", "g2", "be2"))
        srcs, dsts, tgts = (sb(n, [128, GROUPS * T], I32) for n in ("srcs", "dsts", "tgts"))
        dstf = sb("dstf", [128, GROUPS * T])

        def load_indices(eng, to, indices, ready):
            full = indices[0:FULL * ROWS].rearrange("(g p c) -> p g c", p=128, c=T)
            eng.dma_start(to[:, 0:FULL * T].rearrange("p (g c) -> p g c", c=T), full).then_inc(ready, 16)
            eng.dma_start(to[0:TAIL, FULL * T:], indices[FULL * ROWS:NODES].rearrange("(p c) -> p c", c=T))\
               .then_inc(ready, 16)

        with ExitStack() as c2:
            sem, pair = semaphores(c2)
            s_const = sem("setup_const")
            s_w0 = sem("setup_w0")
            s_idx = sem("setup_idx")
            s_zero = [sem(f"setup_zero{k}") for k in range(9)]
            s_clear = sem("setup_clear")
            s_t = sem("setup_wT")
            s_tc = sem("setup_wT_copied")
            s_gv = sem("setup_gvec")
            s_masks = sem("setup_masks")
            s_done = sem("setup_dve")
            block = c2.enter_context(nc.Block())

            @block.sync
            def _(sp):
                sp.dma_start(w0[:, :], a["W"]).then_inc(s_w0, 16)
                sp.dma_start(glob[:, :], a["glob"][0, :].rearrange("(k a) -> k a", a=1)).then_inc(s_w0, 16)
                sp.wait_ge(s_clear, 3)
                load_indices(sp, dsts, a["dst"], s_idx)

            @block.scalar
            def _(act):
                act.wait_ge(s_clear, 1)
                clear(act, edge_sum[0], zeros[:, 0:T * WM], s_zero)
                wait_clear(act, s_zero)

            @block.gpsimd
            def _(pool):
                pool.memset(ident[:, :], 0.0).then_inc(s_const, 1)
                pool.memset(early[:, :, :], 1.0).then_inc(s_const, 1)
                pool.memset(heads[:, :], DK ** -0.5).then_inc(s_const, 1)
                pool.memset(ones[:, :], 1.0).then_inc(s_const, 1)
                pool.memset(eps[:, :], EPS).then_inc(s_const, 1)
                pool.iota(dumprow[:, :], pattern=[[128, T]], base=DUMP, channel_multiplier=1,
                          allow_small_or_imprecise_dtypes=True).then_inc(s_const, 1)
                pool.wait_ge(s_const, 6)
                pool.affine_select(out=ident[:, :], in_=ident[:, :], compare_op=ALU.not_equal, fill=1.0, base=0,
                                   pattern=[[-1, 128]], channel_multiplier=1).then_inc(s_masks, 1)
                pool.affine_select(out=early[:, NEAR - 1, :], in_=early[:, NEAR - 1, :], compare_op=ALU.is_gt, fill=0.0, base=0,
                                   pattern=[[-1, 128]], channel_multiplier=1).then_inc(s_masks, 1)
                pool.affine_select(out=heads[:, :], in_=heads[:, :], compare_op=ALU.is_ge, fill=0.0, base=0,
                                   pattern=[[-DK, HEADS]], channel_multiplier=1).then_inc(s_masks, 1)
                pool.wait_ge(s_masks, 3)
                pool.affine_select(out=heads[:, :], in_=heads[:, :], compare_op=ALU.is_ge, fill=0.0, base=DK - 1,
                                   pattern=[[DK, HEADS]], channel_multiplier=-1).then_inc(s_masks, 1)

            @block.vector
            def _(dve):
                dve.memset(zeros[:, :], 0.0).then_inc(s_clear, 1)
                dve.memset(srcs[:, :], 0.0).then_inc(s_clear, 1)
                dve.memset(dsts[:, :], 0.0).then_inc(s_clear, 1)
                dve.memset(tgts[:, :], 0.0).then_inc(s_done, 1)
                for k, (t, n) in enumerate(((wxT, 128), (weT, 128), (wgT, 64))):
                    dve.wait_ge(s_t, k + 1)
                    dve.tensor_copy(t[:, :], banks[0:n, k, 0:128]).then_inc(s_tc, 1)
                dve.wait_ge(s_gv, 1)
                dve.tensor_copy(gvec[:, :], banks[:, 3, 0:1]).then_inc(s_done, 1)
                dve.wait_ge(s_idx, 32)
                dve.tensor_copy(dstf[:, :], dsts[:, :]).then_inc(s_done, 1)

            @block.tensor
            def _(pe):
                pe.wait_ge(s_w0, 32)
                pe.wait_ge(s_masks, 1)
                for k, n in enumerate((128, 128, 64)):
                    pe.transpose(banks[0:n, k, 0:128], w0[:, 128 * k:128 * k + n], ident[:, :]).then_inc(s_t, 1)
                pe.wait_ge(s_tc, 3)
                pe.matmul(banks[:, 3, 0:1], wgT[:, :], glob[:, :], start=True, stop=True).then_inc(s_gv, 1)

        def carry_wait(eng, passed):
            eng.sem_inc(passed, 1)

        dcol = [sb(f"dcol{u}", [128, T]) for u in range(2)]
        same = [sb(f"same{u}", [128, T, T, 128]) for u in range(2)]
        tgt = [sb(f"tgt{u}", [128, T], I32) for u in range(2)]

        def copy_dst(dve, g, ready):
            dve.tensor_copy(dcol[g.u][0:g.P, :], dstf[0:g.P, bass.ds(g.n * T, T)]).then_inc(ready, 1)

        def spread_dst(pe, g, bank, ready):
            P = g.P
            for c in range(T):
                last = pe.transpose(bank[0:P, c * 128:c * 128 + P], dcol[g.u][0:P, c:c + 1].to_broadcast([P, P]),
                                    ident[0:P, 0:P])
            last.then_inc(ready, 1)

        def build_same(dve, g, bank, ready):
            P = g.P
            seen = tiles(bank, P)[:, :, 0:P]
            for c in range(T):
                dve.tensor_scalar(same[g.u][0:P, c, :, 0:P], seen, dcol[g.u][0:P, c:c + 1], None, ALU.is_equal)\
                   .then_inc(ready, 1)

        def sum_same(pe, g, rows, width, sums, ready):
            P = g.P
            for b in range(T):
                to = sums[0:P, b // 2, (b % 2) * width:(b % 2 + 1) * width]
                for c in range(T):
                    last = pe.matmul(to, same[g.u][0:P, c, b, 0:P], rows[0:P, c, 0:width],
                                     start=(c == 0), stop=(c == T - 1))
            last.then_inc(ready, 1)

        with ExitStack() as c2:
            sem, pair = semaphores(c2)
            feat = [sb(f"feat{u}", [128, T, WM]) for u in range(2)]
            sums = [sb(f"esums{u}", [128, T * WM]) for u in range(2)]
            junk = sb("junk", [128, T * (T + 1) // 2, 128])
            before = [sb(f"before{u}", [128, T]) for u in range(2)]
            away = sb("away", [128, T])
            shift = sb("shift", [128, T])
            s_one = sem("e_ones")
            s_feat = pair("e_feat")
            s_dcol = sem("e_dcol")
            s_spread = sem("e_spread")
            s_same = sem("e_same")
            s_near = sem("e_near")
            s_tiles = sem("e_tiles")
            s_before = sem("e_before")
            s_away = sem("e_away")
            s_shift = sem("e_shift")
            s_tgt = sem("e_tgt")
            s_keep = sem("e_keep")
            s_mm = sem("e_summed")
            s_sums = sem("e_sums")
            s_scat = e_scattered
            s_second = [sem(f"e_second{k}") for k in range(3)]
            s_zero = pair("e_zeroed") + [sem("e_zeroed2")]
            s_carry = sem("e_carry")
            s_ld = sem("e_loads")
            loads = [
                (wq[:, :, :], a["Wq"].rearrange("l k m -> k l m")), (wk[:, :, :], a["Wk"].rearrange("l k m -> k l m")),
                (wv[:, :, :], a["Wv"].rearrange("l k m -> k l m")), (wo[:, :, :], a["Wo"].rearrange("l k m -> k l m")),
                (w1[:, :, :], a["W1"].rearrange("l k m -> k l m")),
                (bv[:, :, :], a["bv"].rearrange("(a l) d -> a l d", a=1)),
            ]
            loads += [(w2[:, l, :, :], a["W2"][l, :, :].rearrange("(c k) m -> k c m", k=128)) for l in range(LAYERS)]
            loads += [(t[:, l:l + 1], a[n][l, :].rearrange("(d a) -> d a", a=1)) for t, n in
                      ((bq, "bq"), (bk, "bk"), (b2, "b2"), (g1, "ln1_g"), (be1, "ln1_b")) for l in range(LAYERS)]
            loads += [(b1[:, 2 * l + k:2 * l + k + 1], a["b1"][l, 128 * k:128 * (k + 1)].rearrange("(d a) -> d a", a=1))
                      for l in range(LAYERS) for k in range(2)]
            loads += [(t[:, l, :], a[n][l, :].partition_broadcast(128)) for t, n in
                      ((bo, "bo"), (g2, "ln2_g"), (be2, "ln2_b")) for l in range(LAYERS)]
            block = c2.enter_context(nc.Block())
            ALONE = 14
            PC = 6

            @block.sync
            def _(sp):
                clear(sp, edge_sum[1], zeros[:, 0:T * WM], s_second)
                load_indices(sp, srcs, a["src"], s_ld)
                for to, fr in loads:
                    sp.dma_start(to, fr).then_inc(s_ld, 16)
                clear(sp, attn_sum[0], zeros[:, :], s_zero)
                wait_clear(sp, s_zero)
                sp.wait_ge(s_ld, 16 * (2 + len(loads)))

            @block.scalar
            def _(act):
                def load(g):
                    src = rows_of(a["edge"], g, D).rearrange("p (c f) -> p c f", c=T)
                    act.dma_start(feat[g.u][0:g.P, :, 0:D], src).then_inc(s_feat[g.u], 16)

                act.wait_ge(s_one, 2)
                load(Group(0, 0, 0, 128))
                load(Group(1, 0, 1, 128))

                def step(g):
                    act.wait_ge(s_mm, g.n + 1)
                    if near(g, 2):
                        load(near(g, 2))
                    if from_group(g, 2):
                        act.wait_ge(s_scat[g.u], g.h * (16 * T))
                    act.activation(sums[g.u][0:g.P, :].rearrange("p (k f) -> p k f", k=2),
                                   banks[0:g.P, 2 + 2 * g.u:4 + 2 * g.u, 0:2 * WM], ACT.Copy).then_inc(s_sums, 1)
                over_groups(act, step, first=ALONE)

            @block.gpsimd
            def _(pool):
                def step(g):
                    early_group = isinstance(g.n, int) and g.n < ALONE
                    pool.wait_ge(s_tgt, g.n + 1)
                    pool.wait_ge(s_sums, g.n + 1)
                    if early_group and g.n:
                        p = near(g, -1)
                        pool.wait_ge(s_scat[p.u], (p.h + 1) * (16 * T))
                    if not early_group:
                        pool.wait_ge(s_scat[g.u], g.h * (16 * T))
                    carry_wait(pool, s_carry)
                    to = edge_sum[0 if early_group else g.u]
                    for c in range(T):
                        pool.indirect_dma_start(to, bass.IndirectOffsetOnAxis(tgt[g.u][0:g.P, c:c + 1], 0),
                                                sums[g.u][0:g.P, c * WM:(c + 1) * WM], None, compute_op=ALU.add)\
                            .then_inc(s_scat[g.u], 16)
                    if isinstance(g.n, int) and g.n == ALONE - 1:
                        pool.wait_ge(s_scat[g.u], (g.h + 1) * (16 * T))
                        wait_clear(pool, s_second)
                over_groups(pool, step, first=ALONE)
                pool.wait_ge(s_scat[0], GROUPS // 2 * 16 * T)
                pool.wait_ge(s_scat[1], GROUPS // 2 * 16 * T)

            @block.vector
            def _(dve):
                for u in range(2):
                    dve.memset(feat[u][:, :, D:WM], 1.0).then_inc(s_one, 1)
                copy_dst(dve, Group(0, 0, 0, 128), s_dcol)

                def count(g):
                    P = g.P
                    dve.wait_ge(s_near, T * (g.n + 1))
                    dve.wait_ge(s_tiles, g.n + 1)
                    dve.tensor_tensor(before[g.u][0:P, NEAR:T], before[g.u][0:P, NEAR:T],
                                      banks[0:P, PC, T * g.u + NEAR:T * (g.u + 1)], ALU.add).then_inc(s_before, 1)
                    if from_group(g, 1):
                        dve.wait_ge(s_shift, g.n)
                    dve.tensor_tensor(away[0:P, :], dumprow[0:P, :], dcol[g.u][0:P, :], ALU.subtract)\
                       .then_inc(s_away, 1)

                def shifted(g):
                    P = g.P
                    dve.wait_ge(s_away, g.n + 1)
                    dve.wait_ge(s_before, g.n + 1)
                    if from_group(g, 1):
                        dve.wait_ge(s_tgt, g.n)
                    dve.scalar_tensor_tensor(out=shift[0:P, :], in0=before[g.u][0:P, :], scalar=1.0,
                                             in1=away[0:P, :], op0=ALU.min, op1=ALU.mult).then_inc(s_shift, 1)

                def target(g):
                    P = g.P
                    dve.wait_ge(s_shift, g.n + 1)
                    if from_group(g, 2):
                        dve.wait_ge(s_scat[g.u], g.h * (16 * T))
                        dve.wait_ge(s_keep, g.n - 1)
                    dve.tensor_tensor(tgt[g.u][0:P, :], shift[0:P, :], dcol[g.u][0:P, :], ALU.add).then_inc(s_tgt, 1)

                def keep(g):
                    dve.wait_ge(s_tgt, g.n + 1)
                    dve.tensor_copy(tgts[0:g.P, bass.ds(g.n * T, T)], tgt[g.u][0:g.P, :]).then_inc(s_keep, 1)

                def next_dst(g):
                    if from_group(g, 1):
                        dve.wait_ge(s_tgt, g.n)
                    copy_dst(dve, near(g, 1), s_dcol)

                def large(g, c):
                    P = g.P
                    if c == 0:
                        dve.wait_ge(s_spread, g.n + 1)
                        dve.wait_ge(s_dcol, g.n + 1)
                        if from_group(g, 2):
                            dve.wait_ge(s_mm, g.n - 1)
                            dve.wait_ge(s_tiles, g.n - 1)
                    dve.tensor_scalar(same[g.u][0:P, c, :, 0:P], tiles(banks[:, g.u, :], P)[:, :, 0:P],
                                      dcol[g.u][0:P, c:c + 1], None, ALU.is_equal).then_inc(s_same, 1)

                def count_near(g):
                    P = g.P
                    if from_group(g, 1):
                        dve.wait_ge(s_near, T * g.n)
                    if from_group(g, 2):
                        dve.wait_ge(s_shift, g.n - 1)
                    for c in range(T):
                        b = 0 if c < NEAR else c
                        at = c * (c + 1) // 2
                        dve.scalar_tensor_tensor(out=junk[0:P, at:at + c - b + 1, 0:P],
                                                 in0=tiles(banks[:, g.u, :], P)[:, b:c + 1, 0:P],
                                                 scalar=dcol[g.u][0:P, c:c + 1], in1=early[0:P, NEAR - 1 - (c - b):NEAR, 0:P],
                                                 op0=ALU.is_equal, op1=ALU.mult,
                                                 accum_out=before[g.u][0:P, c:c + 1]).then_inc(s_near, 1)

                def step(g):
                    small = near(g, -1)
                    here = near(g, 0)
                    if here:
                        large(g, 0)
                    if small:
                        count(small)
                    if here:
                        large(g, 1)
                    if small:
                        shifted(small)
                    if here:
                        large(g, 2)
                    if small:
                        target(small)
                    if near(g, 1):
                        next_dst(g)
                    if small:
                        keep(small)
                    if here:
                        large(g, 3)
                        count_near(g)
                over_groups(dve, step, 1, first=ALONE)

            @block.tensor
            def _(pe):
                def spread(g):
                    pe.wait_ge(s_dcol, g.n + 1)
                    if from_group(g, 2):
                        pe.wait_ge(s_near, T * (g.n - 1))
                    spread_dst(pe, g, banks[:, g.u, :], s_spread)

                def count_tiles(g):
                    P = g.P
                    pe.wait_ge(s_same, (g.n + 1) * T)
                    if from_group(g, 2):
                        pe.wait_ge(s_before, g.n - 1)
                    for c in range(NEAR, T):
                        to = banks[0:P, PC, T * g.u + c:T * g.u + c + 1]
                        for b in range(c):
                            last = pe.matmul(to, same[g.u][0:P, b, c, 0:P], ones[0:P, 0:1],
                                             start=(b == 0), stop=(b == c - 1))
                    last.then_inc(s_tiles, 1)

                spread(Group(0, 0, 0, 128))

                def step(g):
                    if near(g, 1):
                        spread(near(g, 1))
                    count_tiles(g)
                    pe.wait_ge(s_same, (g.n + 1) * T)
                    pe.wait_ge(s_feat[g.u], (g.h + 1) * 16)
                    if from_group(g, 2):
                        pe.wait_ge(s_sums, g.n - 1)
                    sum_same(pe, g, feat[g.u], WM, banks[:, 2 + 2 * g.u:4 + 2 * g.u, :], s_mm)
                over_groups(pe, step, first=ALONE)

        class Norm:

            def __init__(self, sem, name, kind):
                self.st = sb(f"norm{kind}st", [128, T, 6])
                self.mv, self.rs, self.nm = ([sb(f"norm{kind}{n}{u}", [128, T, w]) for u in range(2)]
                                             for n, w in (("mv", 2), ("rs", 1), ("nm", 1)))
                self.sd, self.t1, self.t2 = (sb(f"norm{kind}{n}", [128, T]) for n in ("sd", "t1", "t2"))
                self.s_carry = sem(name + "_carry")
                self.s_st = sem(name + "_stats")
                self.s_mv = sem(name + "_meanvar")
                self.s_ln = sem(name + "_lnvar")
                self.s_sd = sem(name + "_root")
                self.s_t1 = sem(name + "_newton1")
                self.s_t2 = sem(name + "_newton2")
                self.s_rs = sem(name + "_rstd")
                self.s_nm = sem(name + "_bias")
                self.s_out = sem(name + "_normed")

        def norm_stats(dve, N, g, y):
            P = g.P
            if from_group(g, 1):
                dve.wait_ge(N.s_mv, g.n)
            for c in range(T):
                last = dve.bn_stats(N.st[0:P, c, :], y[:, c, :])
            last.then_inc(N.s_st, 1)

        def norm_meanvar(dve, N, g):
            P = g.P
            dve.wait_ge(N.s_st, g.n + 1)
            if from_group(g, 2):
                dve.wait_ge(N.s_out, g.n - 1)
            carry_wait(dve, N.s_carry)
            for c in range(T):
                last = dve.bn_aggr(N.mv[g.u][0:P, c, :], N.st[0:P, c, :])
            last.then_inc(N.s_mv, 1)

        def norm_root(act, N, g):
            act.wait_ge(N.s_mv, g.n + 1)
            if from_group(g, 1):
                act.wait_ge(N.s_rs, g.n)
            act.activation(N.sd[0:g.P, :], N.mv[g.u][0:g.P, :, 1], ACT.Sqrt, bias=eps[0:g.P, :]).then_inc(N.s_sd, 1)

        def norm_recip(dve, N, g):
            dve.wait_ge(N.s_sd, g.n + 1)
            dve.reciprocal(N.rs[g.u][0:g.P, :, 0], N.sd[0:g.P, :]).then_inc(N.s_rs, 1)

        def norm_root_exp(act, N, g):
            act.wait_ge(N.s_mv, g.n + 1)
            if from_group(g, 1):
                act.wait_ge(N.s_rs, g.n)
            act.activation(N.t1[0:g.P, :], N.mv[g.u][0:g.P, :, 1], ACT.Ln, bias=eps[0:g.P, :]).then_inc(N.s_ln, 1)
            act.wait_ge(N.s_ln, g.n + 1)
            act.activation(N.sd[0:g.P, :], N.t1[0:g.P, :], ACT.Exp, scale=-0.5).then_inc(N.s_sd, 1)

        def norm_newton(dve, N, g):
            P = g.P
            dve.wait_ge(N.s_sd, g.n + 1)
            dve.scalar_tensor_tensor(out=N.t2[0:P, :], in0=N.mv[g.u][0:P, :, 1], scalar=EPS, in1=N.sd[0:P, :],
                                     op0=ALU.add, op1=ALU.mult).then_inc(N.s_t1, 1)
            dve.wait_ge(N.s_t1, g.n + 1)
            dve.scalar_tensor_tensor(out=N.t2[0:P, :], in0=N.t2[0:P, :], scalar=-0.5, in1=N.sd[0:P, :],
                                     op0=ALU.mult, op1=ALU.mult).then_inc(N.s_t2, 1)
            dve.wait_ge(N.s_t2, g.n + 1)
            dve.scalar_tensor_tensor(out=N.rs[g.u][0:P, :, 0], in0=N.t2[0:P, :], scalar=1.5, in1=N.sd[0:P, :],
                                     op0=ALU.add, op1=ALU.mult).then_inc(N.s_rs, 1)

        def norm_bias(dve, N, g):
            P = g.P
            dve.wait_ge(N.s_rs, g.n + 1)
            dve.scalar_tensor_tensor(out=N.nm[g.u][0:P, :, 0], in0=N.mv[g.u][0:P, :, 0], scalar=-1.0, in1=N.rs[g.u][0:P, :, 0],
                                     op0=ALU.mult, op1=ALU.mult).then_inc(N.s_nm, 1)

        def norm_apply(act, N, g, y, to):
            P = g.P
            act.wait_ge(N.s_nm, g.n + 1)
            for c in range(T):
                last = act.activation(to[:, c, :], y[:, c, :], ACT.Identity, bias=N.nm[g.u][0:P, c, :],
                                      scale=N.rs[g.u][0:P, c, :])
            last.then_inc(N.s_out, 1)

        def norm_apply_dve(dve, N, g, y, to):
            P = g.P
            dve.wait_ge(N.s_rs, g.n + 1)
            for c in range(T):
                last = dve.tensor_scalar(to[:, c, :], y[:, c, :], N.mv[g.u][0:P, c, 0:1], N.rs[g.u][0:P, c, :],
                                         ALU.subtract, ALU.mult)
            last.then_inc(N.s_out, 1)

        with ExitStack() as c2:
            sem, pair = semaphores(c2)
            xr = [sb(f"xr{u}", [128, T, D]) for u in range(2)]
            es = [sb(f"es{u}", [128, T, WM]) for u in range(2)]
            eo = [sb(f"eo{u}", [128, T, WM]) for u in range(2)]
            ea = [sb(f"ea{u}", [128, T, WM]) for u in range(2)]
            cnt = sb("cnt", [128, T])
            rc = sb("rc", [128, T])
            mean = [sb(f"mean{u}", [128, T, D]) for u in range(2)]
            xT = [sb(f"xT{u}", [128, 512]) for u in range(2)]
            mT = sb("mT", [128, 512])
            ab = sb("ab", [128, 512])
            ex = sb("ex", [128, 512])
            pos = sb("pos", [128, 512])
            soft = sb("soft", [128, 512])
            yT = [sb(f"yT{u}", [128, 512]) for u in range(2)]
            o = [sb(f"o{u}", [128, T, D]) for u in range(2)]
            N = Norm(sem, "n0", 1)
            s_x, s_es, s_st = pair("z_x"), pair("z_es"), pair("z_stored")
            s_ea, s_cnt, s_rc, s_mean = sem("z_ea"), sem("z_cnt"), sem("z_rc"), sem("z_mean")
            s_xt, s_mt, s_xT, s_mT = sem("z_xt"), sem("z_mt"), sem("z_xT"), sem("z_mT")
            s_h, s_ab, s_ex, s_lg = sem("z_h"), sem("z_abs"), sem("z_exp"), sem("z_log")
            s_pos, s_soft, s_yT, s_back = sem("z_pos"), sem("z_soft"), sem("z_yT"), sem("z_back")
            block = c2.enter_context(nc.Block())
            PX, PM, PH, PL, PB = 0, 1, 2, 3, 4

            LAG = 5

            @block.sync
            def _(sp):
                def step(g):
                    if near(g, 0):
                        if from_group(g, 2):
                            sp.wait_ge(s_ea, g.n - 1)
                        for to, fr in ((es, edge_sum[0]), (eo, edge_sum[1])):
                            sp.dma_start(to[g.u][0:g.P, :, :],
                                         rows_of(fr, g, WM).rearrange("p (c f) -> p c f", c=T))\
                              .then_inc(s_es[g.u], 16)
                        if from_group(g, 2):
                            sp.wait_ge(s_xt, g.n - 1)
                        sp.dma_start(xr[g.u][0:g.P, :, :], rows_of(a["x"], g, D).rearrange("p (c f) -> p c f", c=T))\
                          .then_inc(s_x[g.u], 16)
                over_groups(sp, step)

            @block.gpsimd
            def _(pool):
                def add(g):
                    P = g.P
                    pool.wait_ge(s_es[g.u], (g.h + 1) * 32)
                    if from_group(g, 2):
                        pool.wait_ge(s_mean, g.n - 1)
                    pool.tensor_tensor(ea[g.u][0:P, :, :], es[g.u][0:P, :, :], eo[g.u][0:P, :, :], ALU.add)\
                        .then_inc(s_ea, 1)

                def means(g):
                    P = g.P
                    pool.wait_ge(s_rc, g.n + 1)
                    if from_group(g, 2):
                        pool.wait_ge(s_mt, g.n - 1)
                    pool.tensor_tensor(mean[g.u][0:P, :, :], ea[g.u][0:P, :, 0:D],
                                       rc[0:P, :].unsqueeze(2).to_broadcast([P, T, D]), ALU.mult).then_inc(s_mean, 1)

                def residual(g):
                    W = T * g.P
                    pool.wait_ge(s_soft, g.n + 1)
                    pool.wait_ge(s_xT, g.n + 1)
                    if from_group(g, 2):
                        pool.wait_ge(s_back, g.n - 1)
                    pool.tensor_tensor(yT[g.u][:, 0:W], soft[:, 0:W], xT[g.u][:, 0:W], ALU.add).then_inc(s_yT, 1)

                def step(g):
                    for d, part in ((0, add), (-3, residual), (0, means)):
                        if near(g, d):
                            part(near(g, d))
                over_groups(pool, step, LAG)

            @block.tensor
            def _(pe):
                def turn(g):
                    P = g.P
                    pe.wait_ge(s_x[g.u], (g.h + 1) * 16)
                    if from_group(g, 1):
                        pe.wait_ge(s_xT, g.n)
                    for c in range(T):
                        last = pe.transpose(banks[:, PX, c * P:(c + 1) * P], xr[g.u][0:P, c, :], ident[0:P, 0:P])
                    last.then_inc(s_xt, 1)
                    pe.wait_ge(s_mean, g.n + 1)
                    if from_group(g, 1):
                        pe.wait_ge(s_mT, g.n)
                    for c in range(T):
                        last = pe.transpose(banks[:, PM, c * P:(c + 1) * P], mean[g.u][0:P, c, :], ident[0:P, 0:P])
                    last.then_inc(s_mt, 1)

                def product(g):
                    W = T * g.P
                    pe.wait_ge(s_xT, g.n + 1)
                    if from_group(g, 1):
                        pe.wait_ge(s_pos, g.n)
                    pe.matmul(banks[:, PH, 0:W], wxT[:, :], xT[g.u][:, 0:W], start=True, stop=False)
                    pe.wait_ge(s_mT, g.n + 1)
                    pe.matmul(banks[:, PH, 0:W], weT[:, :], mT[:, 0:W], start=False, stop=True).then_inc(s_h, 1)

                def back(g):
                    P = g.P
                    pe.wait_ge(s_yT, g.n + 1)
                    if from_group(g, 2):
                        pe.wait_ge(N.s_out, g.n - 1)
                    for c in range(T):
                        last = pe.transpose(banks[0:P, PB + g.u, c * 128:(c + 1) * 128], yT[g.u][:, c * P:(c + 1) * P],
                                            ident[:, :])
                    last.then_inc(s_back, 1)

                def step(g):
                    if near(g, -1):
                        turn(near(g, -1))
                    if near(g, -3):
                        back(near(g, -3))
                    if near(g, -1):
                        product(near(g, -1))
                over_groups(pe, step, LAG)

            @block.scalar
            def _(act):
                def turn(g):
                    W = T * g.P
                    act.wait_ge(s_xt, g.n + 1)
                    if from_group(g, 2):
                        act.wait_ge(s_yT, g.n - 1)
                    act.activation(xT[g.u][:, 0:W], banks[:, PX, 0:W], ACT.Copy).then_inc(s_xT, 1)

                def absolute(g):
                    W = T * g.P
                    act.wait_ge(s_h, g.n + 1)
                    if from_group(g, 1):
                        act.wait_ge(s_ex, g.n)
                    act.activation(ab[:, 0:W], banks[:, PH, 0:W], ACT.Abs, bias=gvec[:, :]).then_inc(s_ab, 1)

                def softplus(g):
                    W = T * g.P
                    act.wait_ge(s_ab, g.n + 1)
                    if from_group(g, 1):
                        act.wait_ge(s_lg, g.n)
                    act.activation(ex[:, 0:W], ab[:, 0:W], ACT.Exp, scale=-1.0).then_inc(s_ex, 1)
                    act.wait_ge(s_ex, g.n + 1)
                    if from_group(g, 1):
                        act.wait_ge(s_soft, g.n)
                    act.activation(banks[:, PL, 0:W], ex[:, 0:W], ACT.Ln, bias=ones[:, 0:1]).then_inc(s_lg, 1)

                def store(g):
                    act.wait_ge(N.s_out, g.n + 1)
                    act.dma_start(rows_of(x1, g, D), o[g.u][0:g.P, :, :].rearrange("p c f -> p (c f)"))\
                       .then_inc(s_st[g.u], 16)

                def norm(g):
                    if from_group(g, 2):
                        act.wait_ge(s_st[g.u], g.h * 16)
                    norm_apply(act, N, g, tiles(banks[:, PB + g.u, :], g.P), o[g.u][0:g.P, :, :])

                def root(g):
                    norm_root_exp(act, N, g)

                def step(g):
                    for d, part in ((-2, absolute), (-5, store), (-4, root), (-1, turn), (-2, softplus), (-4, norm)):
                        if near(g, d):
                            part(near(g, d))
                act.preload_act_table_set("natural_log_exp_and_others")
                over_groups(act, step, LAG)
                for u in range(2):
                    act.wait_ge(s_st[u], GROUPS // 2 * 16)

            @block.vector
            def _(dve):
                def counts(g):
                    P = g.P
                    dve.wait_ge(s_ea, g.n + 1)
                    if from_group(g, 1):
                        dve.wait_ge(s_rc, g.n)
                    dve.tensor_scalar(cnt[0:P, :], ea[g.u][0:P, :, D], 1.0, None, ALU.max).then_inc(s_cnt, 1)
                    dve.wait_ge(s_cnt, g.n + 1)
                    if from_group(g, 1):
                        dve.wait_ge(s_mean, g.n)
                    dve.reciprocal(rc[0:P, :], cnt[0:P, :]).then_inc(s_rc, 1)

                def turn(g):
                    W = T * g.P
                    dve.wait_ge(s_mt, g.n + 1)
                    if from_group(g, 1):
                        dve.wait_ge(s_h, g.n)
                    dve.tensor_copy(mT[:, 0:W], banks[:, PM, 0:W]).then_inc(s_mT, 1)

                def positive(g):
                    W = T * g.P
                    dve.wait_ge(s_ab, g.n + 1)
                    if from_group(g, 1):
                        dve.wait_ge(s_soft, g.n)
                    dve.tensor_scalar(pos[:, 0:W], banks[:, PH, 0:W], gvec[:, 0:1], 0.0, ALU.add, ALU.max)\
                       .then_inc(s_pos, 1)

                def softplus(g):
                    W = T * g.P
                    dve.wait_ge(s_pos, g.n + 1)
                    dve.wait_ge(s_lg, g.n + 1)
                    if from_group(g, 1):
                        dve.wait_ge(s_yT, g.n)
                    dve.scalar_tensor_tensor(out=soft[:, 0:W], in0=pos[:, 0:W], scalar=-math.log(2.0),
                                             in1=banks[:, PL, 0:W], op0=ALU.add, op1=ALU.add).then_inc(s_soft, 1)

                def stats(g):
                    dve.wait_ge(s_back, g.n + 1)
                    norm_stats(dve, N, g, tiles(banks[:, PB + g.u, :], g.P))
                    norm_meanvar(dve, N, g)

                def rstd(g):
                    norm_newton(dve, N, g)
                    norm_bias(dve, N, g)

                def step(g):
                    for d, part in ((0, counts), (-2, positive), (-1, turn), (-4, rstd), (-2, softplus), (-3, stats)):
                        if near(g, d):
                            part(near(g, d))
                over_groups(dve, step, LAG)

        def edges(l, table):
            with ExitStack() as c2:
                sem, pair = semaphores(c2, f"a{l}_")

                isrc = [sb(f"isrc{u}", [128, T], I32) for u in range(2)]
                idst = [sb(f"idst{u}", [128, T], I32) for u in range(2)]
                hs = [sb(f"hs{u}", [128, T, D]) for u in range(2)]
                hd = [sb(f"hd{u}", [128, T, D]) for u in range(2)]
                hsT, hdT, kT, prod = (sb(n, [128, 512]) for n in ("hsT", "hdT", "kT", "prod"))
                clip = sb("clip", [128, T * HEADS])
                vals = sb("vals", [128, T, WA])
                sums = [sb(f"asums{u}", [128, T * WA]) for u in range(2)]
                s_ix, s_it, s_dcol, s_spread, s_same = sem("ix"), sem("it"), sem("dcol"), sem("spread"), sem("same")
                s_gat, s_scat = a_gathered[l], a_scattered[l]
                s_st, s_dt, s_hsT, s_hdT = sem("st"), sem("dt"), sem("hsT"), sem("hdT")
                s_k, s_q, s_v, s_kT, s_prod = sem("k"), sem("q"), sem("v"), sem("kT"), sem("prod")
                s_sc, s_clip, s_w, s_vals = sem("score"), sem("clip"), sem("weight"), sem("vals")
                s_mm, s_sums = sem("summed"), sem("sums")
                s_carry_g, s_carry_s = sem("carry_gather"), sem("carry_scatter")
                block = c2.enter_context(nc.Block())
                PS, PT, PK, PQ, PV, PD = 0, 1, 2, 3, 4, 5
                s_zero = [sem("zeroed")]
                A = banks[:, 6:8, :]
                SC = banks[:, 7, 512 - T * HEADS:512]

                @block.sync
                def _(sp):
                    if l + 1 < LAYERS:
                        clear(sp, attn_sum[l + 1], zeros[:, :], s_zero)
                        wait_clear(sp, s_zero)

                @block.gpsimd
                def _(pool):
                    def gather(g, c):
                        P = g.P
                        if c == 0:
                            pool.wait_ge(s_ix, 2 * (g.n + 1))
                            if from_group(g, 2):
                                pool.wait_ge(s_dt, g.n - 1)
                            carry_wait(pool, s_carry_g)
                        for ix, to in ((isrc, hs), (idst, hd)):
                            pool.indirect_dma_start(to[g.u][0:P, c, :], None, table,
                                                    bass.IndirectOffsetOnAxis(ix[g.u][0:P, c:c + 1], 0))\
                                .then_inc(s_gat[g.u], 16)

                    def scatter(g, c):
                        if c == 0:
                            pool.wait_ge(s_it, g.n + 1)
                            pool.wait_ge(s_sums, g.n + 1)
                            if from_group(g, 1):
                                p = near(g, -1)
                                pool.wait_ge(s_scat[p.u], (p.h + 1) * (16 * T))
                            carry_wait(pool, s_carry_s)
                        pool.indirect_dma_start(attn_sum[l], bass.IndirectOffsetOnAxis(tgt[g.u][0:g.P, c:c + 1], 0),
                                                sums[g.u][0:g.P, c * WA:(c + 1) * WA], None, compute_op=ALU.add)\
                            .then_inc(s_scat[g.u], 16)

                    for c in range(T):
                        gather(Group(0, 0, 0, 128), c)

                    def step(g):
                        for c in range(T):
                            if near(g, 1):
                                gather(near(g, 1), c)
                        for c in range(T):
                            if near(g, -1):
                                scatter(near(g, -1), c)
                    over_groups(pool, step)
                    for c in range(T):
                        scatter(near(Group(GROUPS, 0, 0, 0), -1), c)
                    for u in range(2):
                        pool.wait_ge(s_scat[u], GROUPS // 2 * 16 * T)

                @block.vector
                def _(dve):
                    def indices(g):
                        dve.tensor_copy(isrc[g.u][0:g.P, :], srcs[0:g.P, bass.ds(g.n * T, T)]).then_inc(s_ix, 1)
                        dve.tensor_copy(idst[g.u][0:g.P, :], dsts[0:g.P, bass.ds(g.n * T, T)]).then_inc(s_ix, 1)

                    indices(Group(0, 0, 0, 128))
                    indices(Group(1, 0, 1, 128))

                    def matrix(g):
                        dve.wait_ge(s_spread, g.n + 1)
                        dve.wait_ge(s_dcol, g.n + 1)
                        if from_group(g, 2):
                            dve.wait_ge(s_mm, g.n - 1)
                        build_same(dve, g, banks[:, PD, :], s_same)
                        if near(g, 1):
                            if from_group(g, 1):
                                dve.wait_ge(s_same, T * g.n)
                                dve.wait_ge(s_spread, g.n)
                            copy_dst(dve, near(g, 1), s_dcol)

                    copy_dst(dve, Group(0, 0, 0, 128), s_dcol)
                    matrix(Group(0, 0, 0, 128))

                    def step(g):
                        P, W = g.P, T * g.P
                        if from_group(g, 2):
                            dve.wait_ge(s_scat[g.u], g.h * (16 * T))
                        dve.tensor_copy(tgt[g.u][0:P, :], tgts[0:P, bass.ds(g.n * T, T)]).then_inc(s_it, 1)
                        dve.wait_ge(s_gat[g.u], (g.h + 1) * (32 * T))
                        if near(g, 2):
                            indices(near(g, 2))
                        dve.wait_ge(s_dt, g.n + 1)
                        if from_group(g, 1):
                            dve.wait_ge(s_q, g.n)
                        dve.tensor_copy(hdT[:, 0:W], banks[:, PT, 0:W]).then_inc(s_hdT, 1)
                        if near(g, 1):
                            matrix(near(g, 1))
                        dve.wait_ge(s_q, g.n + 1)
                        dve.wait_ge(s_kT, g.n + 1)
                        if from_group(g, 1):
                            dve.wait_ge(s_sc, g.n)
                        dve.scalar_tensor_tensor(out=prod[:, 0:W], in0=banks[:, PQ, 0:W], scalar=bq[:, l:l + 1],
                                                 in1=kT[:, 0:W], op0=ALU.add, op1=ALU.mult).then_inc(s_prod, 1)
                        dve.wait_ge(s_sc, g.n + 1)
                        if from_group(g, 1):
                            dve.wait_ge(s_w, g.n)
                        dve.tensor_scalar(clip[0:P, :], SC[0:P, :], -5.0, 5.0, ALU.max, ALU.min).then_inc(s_clip, 1)
                        dve.wait_ge(s_w, g.n + 1)
                        dve.wait_ge(s_v, g.n + 1)
                        weight = vals[0:P, :, D:WA].unsqueeze(3).to_broadcast([P, T, HEADS, DK])
                        dve.tensor_tensor(vals[0:P, :, 0:D].rearrange("p c (h k) -> p c h k", h=HEADS),
                                          banks[0:P, PV, :].rearrange("p (c h k) -> p c h k", c=T, h=HEADS),
                                          weight, ALU.mult).then_inc(s_vals, 1)
                    over_groups(dve, step)

                @block.scalar
                def _(act):
                    def weigh(g):
                        P, W = g.P, T * g.P
                        act.wait_ge(s_st, g.n + 1)
                        if from_group(g, 1):
                            act.wait_ge(s_v, g.n)
                        act.activation(hsT[:, 0:W], banks[:, PS, 0:W], ACT.Copy).then_inc(s_hsT, 1)
                        act.wait_ge(s_k, g.n + 1)
                        if from_group(g, 1):
                            act.wait_ge(s_prod, g.n)
                        act.activation(kT[:, 0:W], banks[:, PK, 0:W], ACT.Identity, bias=bk[:, l:l + 1])\
                           .then_inc(s_kT, 1)

                    def exponential(g):
                        P = g.P
                        act.wait_ge(s_clip, g.n + 1)
                        if from_group(g, 1):
                            act.wait_ge(s_mm, g.n)
                        act.activation(vals[0:P, :, D:WA], clip[0:P, :].rearrange("p (c h) -> p c h", c=T), ACT.Exp)\
                           .then_inc(s_w, 1)

                    def keep_sums(g):
                        P = g.P
                        act.wait_ge(s_mm, g.n + 1)
                        if from_group(g, 2):
                            act.wait_ge(s_scat[g.u], g.h * (16 * T))
                        act.activation(sums[g.u][0:P, :].rearrange("p (k f) -> p k f", k=2), A[0:P, :, 0:2 * WA],
                                       ACT.Copy).then_inc(s_sums, 1)

                    def step(g):
                        for d, part in ((0, weigh), (-1, keep_sums), (0, exponential)):
                            if near(g, d):
                                part(near(g, d))
                    over_groups(act, step, 1)

                @block.tensor
                def _(pe):
                    def spread(g):
                        pe.wait_ge(s_dcol, g.n + 1)
                        if from_group(g, 1):
                            pe.wait_ge(s_same, T * g.n)
                        spread_dst(pe, g, banks[:, PD, :], s_spread)

                    def turn(g):
                        P = g.P
                        pe.wait_ge(s_gat[g.u], (g.h + 1) * (32 * T))
                        if from_group(g, 1):
                            pe.wait_ge(s_hsT, g.n)
                            pe.wait_ge(s_hdT, g.n)
                        for bank, h, done in ((PS, hs, s_st), (PT, hd, s_dt)):
                            for c in range(T):
                                last = pe.transpose(banks[:, bank, c * P:(c + 1) * P], h[g.u][0:P, c, :],
                                                    ident[0:P, 0:P])
                            last.then_inc(done, 1)

                    def products(g):
                        P, W = g.P, T * g.P
                        pe.wait_ge(s_hsT, g.n + 1)
                        if from_group(g, 1):
                            pe.wait_ge(s_kT, g.n)
                        pe.matmul(banks[:, PK, 0:W], wk[:, l, :], hsT[:, 0:W], start=True, stop=True).then_inc(s_k, 1)
                        pe.wait_ge(s_hdT, g.n + 1)
                        if from_group(g, 1):
                            pe.wait_ge(s_prod, g.n)
                        pe.matmul(banks[:, PQ, 0:W], wq[:, l, :], hdT[:, 0:W], start=True, stop=True).then_inc(s_q, 1)
                        if from_group(g, 1):
                            pe.wait_ge(s_vals, g.n)
                        for c in range(T):
                            to = banks[0:P, PV, c * 128:(c + 1) * 128]
                            pe.matmul(to, hsT[:, c * P:(c + 1) * P], wv[:, l, :], start=True, stop=False)
                            last = pe.matmul(to, ones[0:1, 0:P], bv[:, l, :], start=False, stop=True)
                        last.then_inc(s_v, 1)

                    def scores(g):
                        P = g.P
                        pe.wait_ge(s_prod, g.n + 1)
                        if from_group(g, 1):
                            pe.wait_ge(s_clip, g.n)
                            pe.wait_ge(s_sums, g.n)
                        for c in range(T):
                            last = pe.matmul(SC[0:P, c * HEADS:(c + 1) * HEADS], prod[:, c * P:(c + 1) * P],
                                             heads[:, :], start=True, stop=True)
                        last.then_inc(s_sc, 1)

                    def sums_of(g):
                        pe.wait_ge(s_vals, g.n + 1)
                        pe.wait_ge(s_same, T * (g.n + 1))
                        pe.wait_ge(s_clip, g.n + 1)
                        if from_group(g, 1):
                            pe.wait_ge(s_sums, g.n)
                        sum_same(pe, g, vals, WA, A, s_mm)

                    spread(Group(0, 0, 0, 128))

                    def step(g):
                        for d, part in ((1, spread), (0, turn), (-1, sums_of), (0, products), (0, scores)):
                            if near(g, d):
                                part(near(g, d))
                    over_groups(pe, step, 1)

        def nodes(l, table, to_dram, last_layer):
            with ExitStack() as c2:
                sem, pair = semaphores(c2, f"n{l}_")

                ag = [sb(f"ag{u}", [128, T, WA]) for u in range(2)]
                hr = [sb(f"hr{u}", [128, T, D]) for u in range(2)]
                xs = [sb(f"xs{u}", [128, T, D]) for u in range(2)]
                z, rz = sb("z", [128, T, HEADS]), sb("rz", [128, T, HEADS])
                at = [sb(f"at{u}", [128, T, D]) for u in range(2)]
                hb = [sb(f"hb{u}", [128, T, D]) for u in range(2)]
                atT = sb("atT", [128, 512])
                y, xh = (sb(n, [128, T, D]) for n in ("y", "xh"))
                h1T = [sb(f"h1T{u}", [128, 512]) for u in range(2)]
                r0, r1, y2T = (sb(n, [128, 512]) for n in ("r0", "r1", "y2T"))
                xo, sg, xb = (sb(n, [128, T, D]) for n in ("xo", "sg", "xb"))
                res = [sb(f"res{u}", [128, T, D]) for u in range(2)]
                o = [sb(f"o{u}", [128, T, D]) for u in range(2)]
                N1, N2 = Norm(sem, f"n{l}a", 1), Norm(sem, f"n{l}b", 2)
                N3 = Norm(sem, f"n{l}c", 3) if last_layer else None
                s_ag, s_hr, s_xs, s_st = pair("ag"), pair("hr"), pair("xs"), pair("stored")
                s_z, s_rz, s_at, s_hb = sem("z"), sem("rz"), sem("at"), sem("hb")
                s_att, s_atT, s_wo, s_y = sem("att"), sem("atT"), sem("wo"), sem("y")
                s_xt, s_h1T, s_w1, s_r0, s_r1 = sem("xt"), sem("h1T"), sem("w1"), sem("r0"), sem("r1")
                s_w2, s_y2T, s_back, s_sg, s_o, s_xb = (sem(n) for n in ("w2", "y2T", "back", "sg", "o", "xb"))
                block = c2.enter_context(nc.Block())
                PA, PW, PX, PR0, PR1, PF, PB = range(7)
                out_ready = N3.s_out if last_layer else s_o

                LAG = 7

                @block.sync
                def _(sp):
                    def step(g):
                        if near(g, 0):
                            if from_group(g, 2):
                                sp.wait_ge(s_at, g.n - 1)
                            sp.dma_start(ag[g.u][0:g.P, :, :],
                                         rows_of(attn_sum[l], g, WA).rearrange("p (c f) -> p c f", c=T))\
                              .then_inc(s_ag[g.u], 16)
                            if from_group(g, 2):
                                sp.wait_ge(s_hb, g.n - 1)
                            sp.dma_start(hr[g.u][0:g.P, :, :], rows_of(table, g, D).rearrange("p (c f) -> p c f", c=T))\
                              .then_inc(s_hr[g.u], 16)
                        p = near(g, -4)
                        if last_layer and p:
                            if from_group(p, 2):
                                sp.wait_ge(s_xb, p.n - 1)
                            sp.dma_start(xs[p.u][0:p.P, :, :], rows_of(x1, p, D).rearrange("p (c f) -> p c f", c=T))\
                              .then_inc(s_xs[p.u], 16)
                    over_groups(sp, step, LAG)

                @block.gpsimd
                def _(pool):
                    def divide(g):
                        P = g.P
                        pool.wait_ge(s_rz, g.n + 1)
                        if from_group(g, 2):
                            pool.wait_ge(s_att, g.n - 1)
                        pool.tensor_tensor(at[g.u][0:P, :, :].rearrange("p c (h k) -> p c h k", h=HEADS),
                                           ag[g.u][0:P, :, 0:D].rearrange("p c (h k) -> p c h k", h=HEADS),
                                           rz[0:P, :, :].unsqueeze(3).to_broadcast([P, T, HEADS, DK]), ALU.mult)\
                            .then_inc(s_at, 1)
                        pool.wait_ge(s_hr[g.u], (g.h + 1) * 16)
                        if from_group(g, 2):
                            pool.wait_ge(s_y, g.n - 1)
                        pool.tensor_tensor(hb[g.u][0:P, :, :], hr[g.u][0:P, :, :],
                                           bo[0:P, l, :].unsqueeze(1).to_broadcast([P, T, D]), ALU.add)\
                            .then_inc(s_hb, 1)

                    def gain(g):
                        P = g.P
                        if last_layer:
                            pool.wait_ge(s_xs[g.u], (g.h + 1) * 16)
                            if from_group(g, 1):
                                pool.wait_ge(s_o, g.n)
                            pool.tensor_tensor(xb[0:P, :, :], xs[g.u][0:P, :, :],
                                               be2[0:P, l, :].unsqueeze(1).to_broadcast([P, T, D]), ALU.add)\
                                .then_inc(s_xb, 1)
                        pool.wait_ge(N2.s_out, g.n + 1)
                        if from_group(g, 1):
                            pool.wait_ge(s_o, g.n)
                        pool.tensor_tensor(sg[0:P, :, :], xo[0:P, :, :],
                                           g2[0:P, l, :].unsqueeze(1).to_broadcast([P, T, D]), ALU.mult)\
                            .then_inc(s_sg, 1)
                        pool.wait_ge(s_sg, g.n + 1)
                        if last_layer:
                            pool.wait_ge(s_xb, g.n + 1)
                            to, add = res[g.u], xb[0:P, :, :]
                        else:
                            to, add = o[g.u], be2[0:P, l, :].unsqueeze(1).to_broadcast([P, T, D])
                        if from_group(g, 2):
                            if last_layer:
                                pool.wait_ge(N3.s_out, g.n - 1)
                            else:
                                pool.wait_ge(s_st[g.u], g.h * 16)
                        pool.tensor_tensor(to[0:P, :, :], sg[0:P, :, :], add, ALU.add).then_inc(s_o, 1)

                    def step(g):
                        if near(g, 0):
                            divide(g)
                        if near(g, -4):
                            gain(near(g, -4))
                    over_groups(pool, step, LAG)

                @block.tensor
                def _(pe):
                    def attn(g):
                        P = g.P
                        pe.wait_ge(s_at, g.n + 1)
                        if from_group(g, 1):
                            pe.wait_ge(s_atT, g.n)
                        for c in range(T):
                            last = pe.transpose(banks[:, PA, c * P:(c + 1) * P], at[g.u][0:P, c, :], ident[0:P, 0:P])
                        last.then_inc(s_att, 1)

                    def project(g):
                        P = g.P
                        pe.wait_ge(s_atT, g.n + 1)
                        if from_group(g, 1):
                            pe.wait_ge(s_y, g.n)
                        for c in range(T):
                            last = pe.matmul(banks[0:P, PW, c * 128:(c + 1) * 128], atT[:, c * P:(c + 1) * P],
                                             wo[:, l, :], start=True, stop=True)
                        last.then_inc(s_wo, 1)

                    def turn(g):
                        P = g.P
                        pe.wait_ge(N1.s_out, g.n + 1)
                        if from_group(g, 1):
                            pe.wait_ge(s_h1T, g.n)
                        for c in range(T):
                            last = pe.transpose(banks[:, PX, c * P:(c + 1) * P], xh[0:P, c, :], ident[0:P, 0:P])
                        last.then_inc(s_xt, 1)

                    def up(g):
                        W = T * g.P
                        pe.wait_ge(s_h1T, g.n + 1)
                        for k, (bank, used) in enumerate(((PR0, s_r0), (PR1, s_r1))):
                            if from_group(g, 1):
                                pe.wait_ge(used, g.n)
                            pe.matmul(banks[:, bank, 0:W], w1[:, l, 128 * k:128 * (k + 1)], h1T[g.u][:, 0:W],
                                      start=True, stop=True).then_inc(s_w1, 1)

                    def down(g):
                        W = T * g.P
                        pe.wait_ge(s_r0, g.n + 1)
                        if from_group(g, 1):
                            pe.wait_ge(s_y2T, g.n)
                        pe.matmul(banks[:, PF, 0:W], w2[:, l, 0, :], r0[:, 0:W], start=True, stop=False)
                        pe.wait_ge(s_r1, g.n + 1)
                        pe.matmul(banks[:, PF, 0:W], w2[:, l, 1, :], r1[:, 0:W], start=False, stop=True)\
                          .then_inc(s_w2, 1)

                    def back(g):
                        P = g.P
                        pe.wait_ge(s_y2T, g.n + 1)
                        if from_group(g, 2):
                            pe.wait_ge(N2.s_out, g.n - 1)
                        for c in range(T):
                            last = pe.transpose(banks[0:P, PB + g.u, c * 128:(c + 1) * 128], y2T[:, c * P:(c + 1) * P],
                                                ident[:, :])
                        last.then_inc(s_back, 1)

                    def step(g):
                        if last_layer:
                            order = [(-1, attn), (-2, turn), (-1, project), (-3, back), (-2, up), (-2, down)]
                        else:
                            order = [(-1, project), (-2, turn), (-3, back), (-2, up), (0, attn), (-2, down)]
                        for d, part in order:
                            if near(g, d):
                                part(near(g, d))
                    over_groups(pe, step, LAG)

                @block.scalar
                def _(act):
                    def attn(g):
                        W = T * g.P
                        act.wait_ge(s_att, g.n + 1)
                        if from_group(g, 1):
                            act.wait_ge(s_wo, g.n)
                        act.activation(atT[:, 0:W], banks[:, PA, 0:W], ACT.Copy).then_inc(s_atT, 1)

                    def scale(g):
                        W = T * g.P
                        act.wait_ge(s_xt, g.n + 1)
                        if from_group(g, 2):
                            act.wait_ge(s_y2T, g.n - 1)
                        act.activation(h1T[g.u][:, 0:W], banks[:, PX, 0:W], ACT.Identity, bias=be1[:, l:l + 1],
                                       scale=g1[:, l:l + 1]).then_inc(s_h1T, 1)

                    def relu(g):
                        W = T * g.P
                        for k, (r, bank, done) in enumerate(((r0, PR0, s_r0), (r1, PR1, s_r1))):
                            act.wait_ge(s_w1, 2 * g.n + 1 + k)
                            if from_group(g, 1):
                                act.wait_ge(s_w2, g.n)
                            act.activation(r[:, 0:W], banks[:, bank, 0:W], ACT.Relu,
                                           bias=b1[:, 2 * l + k:2 * l + k + 1]).then_inc(done, 1)

                    def root1(g):
                        norm_root(act, N1, g)

                    def root2(g):
                        norm_root(act, N2, g)

                    def root3(g):
                        norm_root(act, N3, g)

                    def store(g):
                        act.wait_ge(out_ready, g.n + 1)
                        act.dma_start(rows_of(to_dram, g, D), o[g.u][0:g.P, :, :].rearrange("p c f -> p (c f)"))\
                           .then_inc(s_st[g.u], 16)

                    def norm2(g):
                        if from_group(g, 1):
                            act.wait_ge(s_sg, g.n)
                        norm_apply(act, N2, g, tiles(banks[:, PB + g.u, :], g.P), xo[0:g.P, :, :])

                    def norm3(g):
                        if from_group(g, 2):
                            act.wait_ge(s_st[g.u], g.h * 16)
                        norm_apply(act, N3, g, res[g.u][0:g.P, :, :], o[g.u][0:g.P, :, :])

                    if last_layer:
                        order = [(-6, norm3), (-1, attn), (-2, scale), (-4, norm2), (-7, store), (-2, relu),
                                 (-5, root3), (-1, root1), (-3, root2)]
                    else:
                        order = [(-6, store), (-1, attn), (-2, scale), (-4, norm2), (-1, root1), (-2, relu),
                                 (-3, root2)]

                    def step(g):
                        for d, part in order:
                            if near(g, d):
                                part(near(g, d))
                    over_groups(act, step, LAG)
                    for u in range(2):
                        act.wait_ge(s_st[u], GROUPS // 2 * 16)

                @block.vector
                def _(dve):
                    def recip_z(g):
                        P = g.P
                        dve.wait_ge(s_ag[g.u], (g.h + 1) * 16)
                        if from_group(g, 1):
                            dve.wait_ge(s_rz, g.n)
                        dve.tensor_scalar(z[0:P, :, :], ag[g.u][0:P, :, D:WA], 1e-6, None, ALU.add).then_inc(s_z, 1)
                        dve.wait_ge(s_z, g.n + 1)
                        if from_group(g, 1):
                            dve.wait_ge(s_at, g.n)
                        dve.reciprocal(rz[0:P, :, :], z[0:P, :, :]).then_inc(s_rz, 1)

                    def attn_residual(g):
                        P = g.P
                        dve.wait_ge(s_wo, g.n + 1)
                        dve.wait_ge(s_hb, g.n + 1)
                        if from_group(g, 1):
                            dve.wait_ge(N1.s_out, g.n)
                        dve.tensor_tensor(y[0:P, :, :], tiles(banks[:, PW, :], P), hb[g.u][0:P, :, :], ALU.add)\
                           .then_inc(s_y, 1)

                    def stats1(g):
                        dve.wait_ge(s_y, g.n + 1)
                        norm_stats(dve, N1, g, y[0:g.P, :, :])

                    def meanvar1(g):
                        norm_meanvar(dve, N1, g)

                    def meanvar2(g):
                        norm_meanvar(dve, N2, g)

                    def meanvar3(g):
                        norm_meanvar(dve, N3, g)

                    def norm1(g):
                        norm_recip(dve, N1, g)
                        if from_group(g, 1):
                            dve.wait_ge(s_xt, g.n)
                        norm_apply_dve(dve, N1, g, y[0:g.P, :, :], xh[0:g.P, :, :])

                    def residual(g):
                        W = T * g.P
                        dve.wait_ge(s_w2, g.n + 1)
                        dve.wait_ge(s_h1T, g.n + 1)
                        if from_group(g, 1):
                            dve.wait_ge(s_back, g.n)
                        dve.scalar_tensor_tensor(out=y2T[:, 0:W], in0=banks[:, PF, 0:W], scalar=b2[:, l:l + 1],
                                                 in1=h1T[g.u][:, 0:W], op0=ALU.add, op1=ALU.add).then_inc(s_y2T, 1)

                    def stats2(g):
                        dve.wait_ge(s_back, g.n + 1)
                        norm_stats(dve, N2, g, tiles(banks[:, PB + g.u, :], g.P))

                    def rstd2(g):
                        norm_recip(dve, N2, g)
                        norm_bias(dve, N2, g)

                    def stats3(g):
                        dve.wait_ge(s_o, g.n + 1)
                        norm_stats(dve, N3, g, res[g.u][0:g.P, :, :])

                    def rstd3(g):
                        norm_recip(dve, N3, g)
                        norm_bias(dve, N3, g)

                    order = [(-2, norm1), (-4, rstd2), (0, recip_z), (-3, residual), (-1, attn_residual),
                             (-1, stats1), (-1, meanvar1), (-3, stats2), (-3, meanvar2)]
                    if last_layer:
                        order = [(-6, rstd3), (-2, norm1), (-4, rstd2), (0, recip_z), (-3, residual), (-5, stats3),
                                 (-1, attn_residual), (-3, stats2), (-1, stats1), (-5, meanvar3), (-1, meanvar1),
                                 (-3, meanvar2)]

                    def step(g):
                        for d, part in order:
                            if near(g, d):
                                part(near(g, d))
                    over_groups(dve, step, LAG)

        edges(0, x1)
        nodes(0, x1, h1, False)
        edges(1, h1)
        nodes(1, h1, out, True)


_INS = {"x": "x", "src": "src", "dst": "dst", "edge_attr_128": "edge", "L0_gnn_global_feats": "glob", "L0_gnn_W": "W"}
_INS.update({f"L1_gnn_{n}": n for n in ("Wq", "bq", "Wk", "bk", "Wv", "bv", "Wo", "bo", "W1", "b1", "W2", "b2",
                                        "ln1_g", "ln1_b", "ln2_g", "ln2_b")})


def kernel(**inputs):
    import numpy as _np
    import concourse.bacc as _bacc
    from concourse import mybir as _mybir
    from concourse.bass_utils import run_bass_kernel_spmd as _run

    nc = _bacc.Bacc("TRN2", target_bir_lowering=False, num_devices=1)
    arrays, args = {}, {}
    for name, short in _INS.items():
        v = _np.ascontiguousarray(inputs[name])
        arrays[f"in_{name}"] = v
        args[short] = nc.dram_tensor(f"in_{name}", v.shape, _mybir.dt.from_np(v.dtype), kind="ExternalInput").ap()
    out = nc.dram_tensor("out_0", (NODES, D), F32, kind="ExternalOutput").ap()
    program(nc, args, out)
    r = _run(nc, [arrays], core_ids=[0])
    return r.results[0]["out_0"]
```
